# Optimizing a Trainium2 kernel written in Bass

```python
import numpy as np
import jax
import jax.numpy as jnp

def _softmax(x, axis=-1):
    return jax.nn.softmax(x, axis=axis)

def _gelu(x):
    return jax.nn.gelu(x, approximate=True)

def _silu(x):
    return jax.nn.silu(x)

def _sigmoid(x):
    return jax.nn.sigmoid(x)

def _layernorm(x, axis=-1, eps=1e-05):
    m = jnp.mean(x, axis=axis, keepdims=True)
    v = jnp.var(x, axis=axis, keepdims=True)
    return (x - m) / jnp.sqrt(v + eps)

def _scatter_add(tgt, idx, src, axis=0):
    return tgt.at[idx].add(src)

def _segment_sum(src, seg, n):
    return jax.ops.segment_sum(src, seg, n)
kernel_name = 'mk_gnn_resnorm_d1_gnn_r8_697fc6'

def setup_inputs(seed: int=0):
    np.random.seed(seed)
    _w = jnp.asarray

    def _rec_inputs():
        import jax
        import jax.numpy as jnp
        _gk = jax.random.key(seed)
        x = -0.0003713 + 1 * jax.random.normal(jax.random.fold_in(_gk, 1), (6250, 256), jnp.float32)
        src = jax.random.randint(jax.random.fold_in(_gk, 2), (100000,), 0, 6250, jnp.int32)
        dst = jax.random.randint(jax.random.fold_in(_gk, 3), (100000,), 0, 6250, jnp.int32)
        _o = jnp.argsort(dst, stable=True)
        src = src[_o]
        dst = dst[_o]
        return (x, src, dst)
    x, src, dst = _rec_inputs()

    def _L0_gnn_setup():
        import jax, jax.numpy as jnp
        import numpy as np
        import math
        N_NODES = 6250
        N_EDGES = 200000
        C = 256
        H = 8
        HD = C // H

        def _layernorm(x, g, b, eps=1e-05):
            mu = jnp.mean(x, axis=-1, keepdims=True)
            var = jnp.mean(jnp.square(x - mu), axis=-1, keepdims=True)
            return (x - mu) * jax.lax.rsqrt(var + eps) * g + b
        key = jax.random.key(seed)
        ks = jax.random.split(key, 16)
        s = 0.02
        d = {'feat': jax.random.normal(ks[0], (N_NODES, C), jnp.float32), 'edge_src': jax.random.randint(ks[1], (N_EDGES,), 0, N_NODES), 'edge_dst': jax.random.randint(ks[2], (N_EDGES,), 0, N_NODES), 'Wq': jax.random.normal(ks[3], (C, C), jnp.float32) * s, 'bq': jnp.zeros((C,), jnp.float32), 'Wk': jax.random.normal(ks[4], (C, C), jnp.float32) * s, 'bk': jnp.zeros((C,), jnp.float32), 'Wv': jax.random.normal(ks[5], (C, C), jnp.float32) * s, 'bv': jnp.zeros((C,), jnp.float32), 'Wp': jax.random.normal(ks[6], (C, C), jnp.float32) * s, 'bp': jnp.zeros((C,), jnp.float32), 'ln_g': jnp.ones((C,), jnp.float32), 'ln_b': jnp.zeros((C,), jnp.float32), 'W1': jax.random.normal(ks[7], (4 * C, C), jnp.float32) * s, 'b1': jnp.zeros((4 * C,), jnp.float32), 'W2': jax.random.normal(ks[8], (C, 4 * C), jnp.float32) * s, 'b2': jnp.zeros((C,), jnp.float32)}
        return d
    _L0_gnn_all = _L0_gnn_setup()
    _L0_gnn_in = {k: v for k, v in _L0_gnn_all.items() if k in ('Wq', 'bq', 'Wk', 'bk', 'Wv', 'bv', 'Wp', 'bp', 'ln_g', 'ln_b', 'W1', 'b1', 'W2', 'b2')}
    del _L0_gnn_all
    return {'x': x, 'src': src, 'dst': dst, 'L0_gnn_Wq': _L0_gnn_in['Wq'], 'L0_gnn_bq': _L0_gnn_in['bq'], 'L0_gnn_Wk': _L0_gnn_in['Wk'], 'L0_gnn_bk': _L0_gnn_in['bk'], 'L0_gnn_Wv': _L0_gnn_in['Wv'], 'L0_gnn_bv': _L0_gnn_in['bv'], 'L0_gnn_Wp': _L0_gnn_in['Wp'], 'L0_gnn_bp': _L0_gnn_in['bp'], 'L0_gnn_ln_g': _L0_gnn_in['ln_g'], 'L0_gnn_ln_b': _L0_gnn_in['ln_b'], 'L0_gnn_W1': _L0_gnn_in['W1'], 'L0_gnn_b1': _L0_gnn_in['b1'], 'L0_gnn_W2': _L0_gnn_in['W2'], 'L0_gnn_b2': _L0_gnn_in['b2']}

def reference(x, src, dst, L0_gnn_Wq, L0_gnn_bq, L0_gnn_Wk, L0_gnn_bk, L0_gnn_Wv, L0_gnn_bv, L0_gnn_Wp, L0_gnn_bp, L0_gnn_ln_g, L0_gnn_ln_b, L0_gnn_W1, L0_gnn_b1, L0_gnn_W2, L0_gnn_b2):
    import jax
    import jax.numpy as jnp

    def _L0_gnn_ref(feat, edge_src, edge_dst, Wq, bq, Wk, bk, Wv, bv, Wp, bp, ln_g, ln_b, W1, b1, W2, b2):
        import jax, jax.numpy as jnp
        import numpy as np
        import math
        N_NODES = 6250
        N_EDGES = 200000
        C = 256
        H = 8
        HD = C // H

        def _layernorm(x, g, b, eps=1e-05):
            mu = jnp.mean(x, axis=-1, keepdims=True)
            var = jnp.mean(jnp.square(x - mu), axis=-1, keepdims=True)
            return (x - mu) * jax.lax.rsqrt(var + eps) * g + b
        n = feat.shape[0]
        q = (feat @ Wq.T + bq).reshape(n, H, HD)
        k = (feat @ Wk.T + bk).reshape(n, H, HD)
        v = (feat @ Wv.T + bv).reshape(n, H, HD)
        score = jnp.einsum('ehd,ehd->eh', q[edge_dst], k[edge_src])
        score = jnp.clip(score / math.sqrt(HD), -10.0, 10.0)
        smax = jax.ops.segment_max(score, edge_dst, num_segments=n)
        smax = jnp.where(jnp.isfinite(smax), smax, 0.0)
        ex = jnp.exp(score - smax[edge_dst])
        den = jax.ops.segment_sum(ex, edge_dst, num_segments=n)
        alpha = ex / den[edge_dst]
        wv = jax.ops.segment_sum(alpha[:, :, None] * v[edge_src], edge_dst, num_segments=n).reshape(n, C)
        y = wv @ Wp.T + bp
        x = feat + y
        h = _layernorm(x, ln_g, ln_b)
        h = jax.nn.gelu(h @ W1.T + b1, approximate=False) @ W2.T + b2
        return x + h
    x = _layernorm(x + _L0_gnn_ref(x, src, dst, L0_gnn_Wq, L0_gnn_bq, L0_gnn_Wk, L0_gnn_bk, L0_gnn_Wv, L0_gnn_bv, L0_gnn_Wp, L0_gnn_bp, L0_gnn_ln_g, L0_gnn_ln_b, L0_gnn_W1, L0_gnn_b1, L0_gnn_W2, L0_gnn_b2), axis=-1)
    return x

_drawn_inputs = setup_inputs


def setup_inputs(seed=0):
    import zlib

    import numpy as np

    out = dict(_drawn_inputs(seed))
    spreads = {'L0_gnn_bq': (0.0, 0.8),
     'L0_gnn_bk': (0.0, 0.8),
     'L0_gnn_bv': (0.0, 0.504),
     'L0_gnn_bp': (0.0, 0.1),
     'L0_gnn_ln_g': (1.0, 0.6),
     'L0_gnn_ln_b': (0.0, 0.8),
     'L0_gnn_b1': (0.0, 0.485),
     'L0_gnn_b2': (0.0, 0.1)}
    factors = {'L0_gnn_Wq': 8.0, 'L0_gnn_Wk': 8.0, 'L0_gnn_Wv': 4.196, 'L0_gnn_Wp': 2.694}
    for name, (base, spread) in spreads.items():
        noise = np.random.default_rng([zlib.crc32(name.encode()), seed]).standard_normal(out[name].shape)
        drawn = base * np.exp(spread * noise) if base else spread * noise
        out[name] = jnp.asarray(drawn.astype(out[name].dtype))
    for name, factor in factors.items():
        out[name] = (out[name] * factor).astype(out[name].dtype)
    return out
```

```python
import concourse.bass as bass
from concourse import mybir
from contextlib import ExitStack

P = 128
NODES, EDGES, C, H = 6250, 100000, 256, 8
HD = C // H
HIDDEN = 4 * C
TILES_PER_BATCH = 4
BATCHES_PER_GROUP = 3
TPG = TILES_PER_BATCH * BATCHES_PER_GROUP
EDGE_TILES = -(-EDGES // P)
GROUPS = -(-EDGE_TILES // TPG)
GROUPS += GROUPS % 2
BATCHES = GROUPS * BATCHES_PER_GROUP
SLOTS = 2 * BATCHES_PER_GROUP
TURNS = GROUPS // 2
ACC = C + H
TB = 125
NODE_TILES = NODES // TB
SB_TILES = 2
SB = TB * SB_TILES
SUPERBLOCKS = NODE_TILES // SB_TILES
KC = C // P
FC = HIDDEN // P
CLIP = 10.0
SCALE = float(HD) ** -0.5
EPS = 1e-5
NEWTON = 4
ROOT_STEPS = 4 + 3 * NEWTON
ROOT_MAGIC = float(0x5F3759DF)
NO_NODE = 1 << 20


def gnn_program(nc, xT, x, w_qkvT, b_qkv, wpT, bp, ln_gb, w1T, b1, w2T, b2, edge_src, edge_dst, bases, out):
    f32, bf16, i32 = mybir.dt.float32, mybir.dt.bfloat16, mybir.dt.int32
    ALU, ACT, AX = mybir.AluOpType, mybir.ActivationFunctionType, mybir.AxisListType

    kv_dram = nc.dram_tensor("kv_rows", [NODES, 2 * C], f32).ap()
    q_dram = nc.dram_tensor("q_parts", [NODES + P, 3 * C], bf16).ap()
    agg_dram = nc.dram_tensor("agg_rows", [NODES + P, ACC], f32).ap()

    ctx = ExitStack()
    with ctx:
        def sb(name, shape, dt=f32):
            return ctx.enter_context(nc.sbuf_tensor(name, shape, dt))

        def sem(name):
            return ctx.enter_context(nc.semaphore(name))

        iota_row = sb("iota_row", [P, P])
        iota_col = sb("iota_col", [P, 1])
        ident = sb("ident", [P, P])
        zeros16 = sb("zeros16", [P, 3 * C], bf16)
        wqkv_sb = sb("wqkv_sb", [P, KC, 3 * C])
        bqkv_sb = sb("bqkv_sb", [P, 3 * C])
        wp_sb = sb("wp_sb", [P, KC, C])
        w1_sb = sb("w1_sb", [P, KC, HIDDEN])
        w2_sb = sb("w2_sb", [P, FC, C])
        bp_sb = sb("bp_sb", [P, C])
        b2_sb = sb("b2_sb", [P, C])
        lngb_sb = sb("lngb_sb", [P, KC, 2])
        b1_sb = sb("b1_sb", [P, FC])
        bases_sb = sb("bases_sb", [1, GROUPS], i32)
        xT_sb = sb("xT_sb", [P, 2, KC, TB])
        q_full = sb("q_full", [P, 2, C])
        q_rest = sb("q_rest", [P, 2, 2, C])
        q_out = sb("q_out", [P, 2, 3 * C], bf16)
        kv_out = sb("kv_out", [P, 2, 2 * C])
        src_sb = sb("src_sb", [P, 2, TPG], i32)
        dst_sb = sb("dst_sb", [P, 2, TPG + 2], i32)
        dloc = sb("dloc", [P, 2, TPG + 2])
        qwin = sb("qwin", [P, 2, 3 * C], bf16)
        kv = sb("kv", [P, SLOTS, TILES_PER_BATCH, 2 * C])
        onehot = sb("onehot", [P, SLOTS, TILES_PER_BATCH, P])
        onehotT = sb("onehotT", [P, 2, TILES_PER_BATCH * P], bf16)
        prod = sb("prod", [P, 2, TILES_PER_BATCH * C])
        score = sb("score", [P, 2, TILES_PER_BATCH * H])
        clipped = sb("clipped", [P, 2, TILES_PER_BATCH * H])
        ev = sb("ev", [P, BATCHES_PER_GROUP, TILES_PER_BATCH, ACC])
        carry_sel = sb("carry_sel", [P, 2, P])
        acc_sb = sb("acc_sb", [P, 2, ACC])
        agg_in = sb("agg_in", [P, 2, SB_TILES, ACC])
        x_in = sb("x_in", [P, 2, SB_TILES, C])
        den = sb("den", [P, 2, SB_TILES, H])
        rden = sb("rden", [P, 2, SB_TILES, H])
        wv = sb("wv", [P, SB_TILES, C])
        wvT = sb("wvT", [P, SB_TILES, KC, TB])
        x_bp = sb("x_bp", [P, 2, SB_TILES, C])
        x_b2 = sb("x_b2", [P, 2, SB_TILES, C])
        x2 = sb("x2", [P, 2, SB_TILES, C])
        xx = sb("xx", [P, 2, SB_TILES, C])
        hn = sb("hn", [P, SB_TILES, C])
        stats = sb("stats", [P, SB_TILES, 6])
        mv = sb("mv", [P, SB_TILES, 2])
        rstd = sb("rstd", [P, SB_TILES, 5])
        hT = sb("hT", [P, KC, SB])
        hidT = sb("hidT", [P, FC, SB])
        z = sb("z", [P, SB_TILES, C])
        zstats = sb("zstats", [P, SB_TILES, 6])
        zmv = sb("zmv", [P, SB_TILES, 2])
        zrstd = sb("zrstd", [P, SB_TILES, 5])
        y_out = sb("y_out", [P, 2, SB_TILES, C])

        bank = [ctx.enter_context(nc.psum_tensor(f"bank{i}", [P, 512], f32)) for i in range(4)]
        quad = ctx.enter_context(nc.psum_tensor("quad", [P, 4, 512], f32))

        s_w = sem("weights_in")
        s_w3 = sem("weights3_in")
        s_id = sem("ident_steps")
        s_const = sem("constants_ready")
        s_zero = sem("tails_zeroed")
        s_x = [sem(f"xT_in{t}") for t in range(2)]
        s_mm = sem("qkv_done")
        s_qfull = sem("q_biased")
        s_qhi = sem("q_hi_done")
        s_qr1 = sem("q_rest1_done")
        s_qmid = sem("q_mid_done")
        s_qr2 = sem("q_rest2_done")
        s_qlo = sem("q_lo_done")
        s_kvb = sem("kv_biased")
        s_qst = [sem(f"q_stored{t}") for t in range(2)]
        s_kvst = [sem(f"kv_stored{t}") for t in range(2)]
        s_src = [sem(f"src_in{t}") for t in range(2)]
        s_dst = [sem(f"dst_in{t}") for t in range(2)]
        s_qwin = [sem(f"qwin_in{t}") for t in range(2)]
        s_kv = [sem(f"kv_in{t}") for t in range(SLOTS)]
        s_dloc = sem("dloc_ready")
        s_csel = sem("carry_sel_ready")
        s_oh = sem("onehot_ready")
        s_ohT = sem("onehot_transposed")
        s_ohTc = sem("onehotT_copied")
        s_qe = sem("q_rows_ready")
        s_prod = sem("prod_ready")
        s_score = sem("score_ready")
        s_clip = sem("clipped_ready")
        s_exp = sem("exp_ready")
        s_ev = sem("weighted_ready")
        s_acc = sem("batch_summed")
        s_grp = sem("group_summed")
        s_accc = sem("sums_copied")
        s_aggst = sem("sums_stored")
        s3_in = [sem(f"node_rows_in{t}") for t in range(2)]
        s3_den = sem("den_guarded")
        s3_rden = sem("den_inverted")
        s3_wv = sem("wv_ready")
        s3_wvT = sem("wv_transposed")
        s3_wvTc = sem("wvT_copied")
        s3_xbp = sem("x_bp_ready")
        s3_xb2 = sem("x_b2_ready")
        s3_y = sem("y_ready")
        s3_x2 = sem("x2_ready")
        s3_xx = sem("xx_ready")
        s3_st = sem("stats_ready")
        s3_mv = sem("mv_ready")
        s3_rs = sem("rstd_ready")
        s3_hn = sem("hn_ready")
        s3_hTp = sem("h_transposed")
        s3_hT = sem("hT_copied")
        s3_f1 = sem("ffn1_done")
        s3_gelu = sem("gelu_done")
        s3_f2 = sem("ffn2_done")
        s3_z = sem("z_ready")
        s3_zst = sem("zstats_ready")
        s3_zmv = sem("zmv_ready")
        s3_zrs = sem("zrstd_ready")
        s3_out = sem("y_out_ready")
        s3_st_out = [sem(f"out_stored{t}") for t in range(2)]

        block = ctx.enter_context(nc.Block())

        s_gate_pool = sem("gate_pool")
        s_gate_dve = sem("gate_dve")

        def turns(eng, body, count):
            body(0)
            with eng.Fori(1, count - 1) as turn:
                body(turn)
            body(count - 1)

        def exists(n, count):
            return 0 <= n < count if isinstance(n, int) else True

        @block.sync
        def _(sp):
            sp.dma_start(wqkv_sb[:], w_qkvT.rearrange("(k p) n -> p k n", p=P)).then_inc(s_w, 16)
            sp.dma_start(bqkv_sb[:], b_qkv.broadcast_to([P, 3 * C])).then_inc(s_w, 16)

            def load_x(t, turn):
                if exists(turn - 1, NODE_TILES // 2):
                    sp.wait_ge(s_mm, 2 * turn + t - 1)
                sp.dma_start(xT_sb[:, t], xT[:, bass.ds((2 * turn + t) * TB, TB)]
                             .rearrange("(k p) n -> p k n", p=P)).then_inc(s_x[t], 16)

            def store_rows(t, turn):
                row = (2 * turn + t) * TB
                sp.wait_ge(s_qlo, 2 * turn + t + 1)
                sp.dma_start(q_dram[bass.ds(row, TB), :], q_out[0:TB, t]).then_inc(s_qst[t], 16)
                sp.wait_ge(s_kvb, 2 * turn + t + 1)
                sp.dma_start(kv_dram[bass.ds(row, TB), :], kv_out[0:TB, t]).then_inc(s_kvst[t], 16)

            n1 = NODE_TILES // 2
            load_x(0, 0)
            load_x(1, 0)
            sp.dma_start(wp_sb[:], wpT.rearrange("(k p) n -> p k n", p=P)).then_inc(s_w3, 16)
            sp.dma_start(w1_sb[:], w1T.rearrange("(k p) n -> p k n", p=P)).then_inc(s_w3, 16)
            sp.dma_start(w2_sb[:], w2T.rearrange("(k p) n -> p k n", p=P)).then_inc(s_w3, 16)
            sp.dma_start(bp_sb[:], bp.broadcast_to([P, C])).then_inc(s_w3, 16)
            sp.dma_start(b2_sb[:], b2.broadcast_to([P, C])).then_inc(s_w3, 16)
            sp.dma_start(lngb_sb[:], ln_gb).then_inc(s_w3, 16)
            sp.dma_start(b1_sb[:], b1).then_inc(s_w3, 16)
            with sp.Fori(1, n1) as turn:
                for t in range(2):
                    load_x(t, turn)
                for t in range(2):
                    store_rows(t, turn - 1)
            for t in range(2):
                store_rows(t, n1 - 1)
            sp.wait_ge(s_const, 1)
            sp.dma_start(q_dram[NODES:NODES + P, :], zeros16[:]).then_inc(s_zero, 16)
            sp.dma_start(bases_sb[:], bases).then_inc(s_zero, 16)

            sp.wait_ge(s_zero, 32)
            for t in range(2):
                sp.wait_ge(s_qst[t], 16 * n1)

            def load_group(g, t, turn):
                if exists(turn - 1, TURNS):
                    for b in range(BATCHES_PER_GROUP):
                        sp.wait_ge(s_kv[t * BATCHES_PER_GROUP + b], 64 * turn)
                sp.dma_start(src_sb[:, t], edge_src[bass.ds(g, 1), :, :].rearrange("g p n -> (g p) n"))\
                    .then_inc(s_src[t], 16)
                if exists(turn - 1, TURNS):
                    sp.wait_ge(s_dloc, g - 1)
                sp.dma_start(dst_sb[:, t], edge_dst[bass.ds(g, 1), :, :].rearrange("g p n -> (g p) n"))\
                    .then_inc(s_dst[t], 16)
                base = sp.value_load(bases_sb[0:1, bass.ds(g, 1)], min_val=0, max_val=NODES - 1)
                if exists(turn - 1, TURNS):
                    sp.wait_ge(s_qe, BATCHES_PER_GROUP * (g - 1))
                sp.dma_start(qwin[:, t], q_dram[bass.ds(base, P), :]).then_inc(s_qwin[t], 16)

            load_group(0, 0, 0)
            load_group(1, 1, 0)
            with sp.Fori(1, TURNS) as turn:
                for t in range(2):
                    load_group(2 * turn + t, t, turn)

            sp.wait_ge(s_aggst, 16 * GROUPS)

            def load_nodes(t, turn):
                s = 2 * turn + t
                if exists(turn - 1, 1 << 20):
                    sp.wait_ge(s3_wv, s - 1)
                    sp.wait_ge(s3_xb2, s - 1)
                rows = bass.ds(s * SB, SB)
                sp.dma_start(agg_in[0:TB, t], agg_dram[rows, :].rearrange("(a p) n -> p a n", p=TB))\
                    .then_inc(s3_in[t], 16)
                sp.dma_start(x_in[0:TB, t], x[rows, :].rearrange("(a p) n -> p a n", p=TB))\
                    .then_inc(s3_in[t], 16)

            def store_nodes(t, turn):
                s = 2 * turn + t
                sp.wait_ge(s3_out, s + 1)
                sp.dma_start(out[bass.ds(s * SB, SB), :].rearrange("(a p) n -> p a n", p=TB),
                             y_out[0:TB, t]).then_inc(s3_st_out[t], 16)

            load_nodes(0, 0)
            load_nodes(1, 0)
            n3 = SUPERBLOCKS // 2
            with sp.Fori(1, n3) as turn:
                for t in range(2):
                    load_nodes(t, turn)
                    store_nodes(t, turn - 1)
            load_nodes(0, n3)
            store_nodes(0, n3 - 1)
            store_nodes(1, n3 - 1)
            store_nodes(0, n3)
            sp.wait_ge(s3_st_out[0], 16 * (n3 + 1))
            sp.wait_ge(s3_st_out[1], 16 * n3)

        @block.gpsimd
        def _(pool):
            nc.gpsimd.memset(zeros16[:], 0.0).then_inc(s_const, 1)
            nc.gpsimd.iota(iota_row[:], [[1, P]], base=0, channel_multiplier=0,
                           allow_small_or_imprecise_dtypes=True).then_inc(s_const, 1)
            nc.gpsimd.iota(iota_col[:], [[0, 1]], base=0, channel_multiplier=1,
                           allow_small_or_imprecise_dtypes=True).then_inc(s_const, 1)
            nc.gpsimd.memset(ident[:], 0.0).then_inc(s_id, 1)
            nc.gpsimd.memset(carry_sel[:], 0.0).then_inc(s_const, 1)
            nc.gpsimd.memset(acc_sb[:], 0.0).then_inc(s_const, 1)
            pool.wait_ge(s_id, 1)
            nc.gpsimd.affine_select(out=ident[:], in_=ident[:], compare_op=ALU.not_equal, fill=1.0,
                                    base=0, pattern=[[-1, P]], channel_multiplier=1).then_inc(s_const, 1)

            def rest(t, turn):
                n = 2 * turn + t
                pool.wait_ge(s_qhi, n + 1)
                nc.gpsimd.tensor_tensor(q_rest[0:TB, t, 0], q_full[0:TB, t], q_out[0:TB, t, 0:C],
                                        ALU.subtract).then_inc(s_qr1, 1)
                pool.wait_ge(s_qmid, n + 1)
                nc.gpsimd.tensor_tensor(q_rest[0:TB, t, 1], q_rest[0:TB, t, 0], q_out[0:TB, t, C:2 * C],
                                        ALU.subtract).then_inc(s_qr2, 1)

            with pool.Fori(0, NODE_TILES // 2) as turn:
                for t in range(2):
                    rest(t, turn)

            for t in range(2):
                pool.wait_ge(s_kvst[t], 16 * (NODE_TILES // 2))

            def gather(turn):
                for slot in range(SLOTS):
                    t, b = divmod(slot, BATCHES_PER_GROUP)
                    if b == 0:
                        pool.wait_ge(s_src[t], 16 * (turn + 1))
                    if exists(turn - 1, TURNS):
                        pool.wait_ge(s_ev, SLOTS * turn + slot - SLOTS + 1)
                    pool.sem_inc(s_gate_pool, 1)
                    for i in range(TILES_PER_BATCH):
                        col = b * TILES_PER_BATCH + i
                        nc.gpsimd.indirect_dma_start(
                            out=kv[:, slot, i, :], out_offset=None, in_=kv_dram,
                            in_offset=bass.IndirectOffsetOnAxis(ap=src_sb[:, t, col:col + 1], axis=0),
                        ).then_inc(s_kv[slot], 16)

            turns(pool, gather, TURNS)

            def sums(t, turn):
                s = 2 * turn + t
                pool.wait_ge(s3_in[t], 32 * (turn + 1))
                if exists(turn - 1, 1 << 20):
                    pool.wait_ge(s3_x2, s - 1)
                for a in range(SB_TILES):
                    last = nc.gpsimd.tensor_tensor(x_bp[0:TB, t, a], x_in[0:TB, t, a], bp_sb[0:TB], ALU.add)
                last.then_inc(s3_xbp, 1)
                if exists(turn - 1, 1 << 20):
                    pool.wait_ge(s3_xx, s - 1)
                for a in range(SB_TILES):
                    last = nc.gpsimd.tensor_tensor(x_b2[0:TB, t, a], x_in[0:TB, t, a], b2_sb[0:TB], ALU.add)
                last.then_inc(s3_xb2, 1)
                pool.wait_ge(s3_x2, s + 1)
                pool.wait_ge(s3_xb2, s + 1)
                if exists(turn - 1, 1 << 20):
                    pool.wait_ge(s3_z, s - 1)
                nc.gpsimd.tensor_tensor(xx[0:TB, t], x2[0:TB, t], x_b2[0:TB, t], ALU.add).then_inc(s3_xx, 1)

            pool.wait_ge(s_w3, 16 * 7)
            for t in range(2):
                sums(t, 0)
            with pool.Fori(1, SUPERBLOCKS // 2) as turn:
                for t in range(2):
                    sums(t, turn)
            sums(0, SUPERBLOCKS // 2)

        @block.tensor
        def _(pe):
            def project(t, turn):
                n = 2 * turn + t
                pe.wait_ge(s_x[t], 16 * (turn + 1))
                if exists(turn - 1, NODE_TILES // 2):
                    pe.wait_ge(s_kvb, n - 1)
                for k in range(KC):
                    nc.tensor.matmul(bank[2 + t][0:TB, 0:C], xT_sb[:, t, k], wqkv_sb[:, k, 0:C],
                                     start=(k == 0), stop=(k == KC - 1))
                for k in range(KC):
                    last = nc.tensor.matmul(quad[0:TB, t, :], xT_sb[:, t, k], wqkv_sb[:, k, C:3 * C],
                                            start=(k == 0), stop=(k == KC - 1))
                last.then_inc(s_mm, 1)

            pe.wait_ge(s_w, 32)
            for t in range(2):
                project(t, 0)
            with pe.Fori(1, NODE_TILES // 2) as turn:
                for t in range(2):
                    project(t, turn)

            def transposes(n, slot, turn):
                pe.wait_ge(s_oh, n + 1)
                if exists(n - 2, BATCHES):
                    pe.wait_ge(s_ohTc, n - 1)
                for i in range(TILES_PER_BATCH):
                    last = nc.tensor.transpose(bank[slot % 2][:, i * P:(i + 1) * P],
                                               onehot[:, slot, i], ident[:])
                last.then_inc(s_ohT, 1)

            def q_rows(n, slot, turn):
                t, b = divmod(slot, BATCHES_PER_GROUP)
                if b == 0:
                    pe.wait_ge(s_qwin[t], 16 * (turn + 1))
                pe.wait_ge(s_ohTc, n + 1)
                if exists(n - 2, BATCHES):
                    pe.wait_ge(s_prod, n - 1)
                for i in range(TILES_PER_BATCH):
                    rows = quad[:, 2 * (slot % 2) + i // 2, (i % 2) * C:(i % 2 + 1) * C]
                    for part in range(3):
                        last = nc.tensor.matmul(rows, onehotT[:, slot % 2, i * P:(i + 1) * P],
                                                qwin[:, t, part * C:(part + 1) * C],
                                                start=(part == 0), stop=(part == 2))
                last.then_inc(s_qe, 1)

            def sums(n, slot, g):
                t, b = divmod(slot, BATCHES_PER_GROUP)
                pe.wait_ge(s_ev, n + 1)
                if b == 0 and exists(g - 2, GROUPS):
                    pe.wait_ge(s_accc, g - 1)
                for i in range(TILES_PER_BATCH):
                    last = nc.tensor.matmul(bank[2 + t][:, 0:ACC], onehot[:, slot, i], ev[:, b, i],
                                            start=(b == 0 and i == 0), stop=False)
                last.then_inc(s_acc, 1)
                if b == BATCHES_PER_GROUP - 1:
                    if exists(g - 1, GROUPS):
                        pe.wait_ge(s_accc, g)
                    pe.wait_ge(s_csel, g + 1)
                    nc.tensor.matmul(bank[2 + t][:, 0:ACC], carry_sel[:, t], acc_sb[:, 1 - t],
                                     start=False, stop=True).then_inc(s_grp, 1)

            def edges(turn):
                for slot in range(SLOTS):
                    n = SLOTS * turn + slot
                    if exists(n + 1, BATCHES):
                        transposes(n + 1, (slot + 1) % SLOTS, turn)
                    q_rows(n, slot, turn)
                    if exists(n - 2, BATCHES):
                        behind = 2 * turn + (slot - 2) // BATCHES_PER_GROUP
                        sums(n - 2, (slot - 2) % SLOTS, behind)

            pe.wait_ge(s_const, 6)
            pe.wait_ge(s_kvb, NODE_TILES)
            transposes(0, 0, 0)
            turns(pe, edges, TURNS)
            for n in (BATCHES - 2, BATCHES - 1):
                sums(n, n % SLOTS, n // BATCHES_PER_GROUP)

            pe.wait_ge(s_accc, GROUPS)
            pe.wait_ge(s_w3, 16 * 7)

            def transpose_wv(s, t):
                pe.wait_ge(s3_wv, s + 1)
                if exists(s - 1, SUPERBLOCKS):
                    pe.wait_ge(s3_wvTc, s)
                for a in range(SB_TILES):
                    for k in range(KC):
                        last = nc.tensor.transpose(bank[0][:, (a * KC + k) * TB:(a * KC + k + 1) * TB],
                                                   wv[0:TB, a, k * P:(k + 1) * P], ident[0:TB, 0:TB])
                last.then_inc(s3_wvT, 1)

            def project_out(s, t):
                pe.wait_ge(s3_wvTc, s + 1)
                if exists(s - 1, SUPERBLOCKS):
                    pe.wait_ge(s3_x2, s)
                for a in range(SB_TILES):
                    for k in range(KC):
                        last = nc.tensor.matmul(bank[1][0:TB, a * C:(a + 1) * C], wvT[:, a, k],
                                                wp_sb[:, k], start=(k == 0), stop=(k == KC - 1))
                last.then_inc(s3_y, 1)

            def transpose_h(s, t):
                pe.wait_ge(s3_hn, s + 1)
                if exists(s - 1, SUPERBLOCKS):
                    pe.wait_ge(s3_hT, s)
                for k in range(KC):
                    for a in range(SB_TILES):
                        last = nc.tensor.transpose(bank[2][:, k * SB + a * TB:k * SB + (a + 1) * TB],
                                                   hn[0:TB, a, k * P:(k + 1) * P], ident[0:TB, 0:TB])
                last.then_inc(s3_hTp, 1)

            def ffn1(s, t):
                pe.wait_ge(s3_hT, s + 1)
                for pair in range(FC // 2):
                    if pair >= 2 or exists(s - 1, SUPERBLOCKS):
                        pe.wait_ge(s3_gelu, (FC // 2) * s + pair - 1)
                    for j in range(2):
                        f = 2 * pair + j
                        for k in range(KC):
                            last = nc.tensor.matmul(quad[:, pair % 2, j * SB:(j + 1) * SB],
                                                    w1_sb[:, k, f * P:(f + 1) * P], hT[:, k],
                                                    start=(k == 0), stop=(k == KC - 1))
                    last.then_inc(s3_f1, 1)

            def ffn2(s, t, a):
                pe.wait_ge(s3_gelu, (FC // 2) * (s + 1))
                if a == 0 and exists(s - 2, SUPERBLOCKS):
                    pe.wait_ge(s3_z, s - 1)
                for f in range(FC):
                    last = nc.tensor.matmul(quad[0:TB, 2 + t, a * C:(a + 1) * C],
                                            hidT[:, f, a * TB:(a + 1) * TB], w2_sb[:, f],
                                            start=(f == 0), stop=(f == FC - 1))
                last.then_inc(s3_f2, 1)

            def superblock(s, t):
                ffn1(s, t)
                more = exists(s + 1, SUPERBLOCKS)
                if more:
                    transpose_wv(s + 1, 1 - t)
                ffn2(s, t, 0)
                if more:
                    project_out(s + 1, 1 - t)
                ffn2(s, t, 1)
                if more:
                    transpose_h(s + 1, 1 - t)

            transpose_wv(0, 0)
            project_out(0, 0)
            transpose_h(0, 0)
            superblock(0, 0)
            superblock(1, 1)
            with pe.Fori(1, SUPERBLOCKS // 2) as turn:
                for t in range(2):
                    superblock(2 * turn + t, t)
            superblock(SUPERBLOCKS - 1, 0)

        @block.scalar
        def _(act):
            def parts(t, turn):
                n = 2 * turn + t
                act.wait_ge(s_qfull, n + 1)
                if exists(turn - 1, NODE_TILES // 2):
                    act.wait_ge(s_qst[t], 16 * turn)
                    act.wait_ge(s_qr2, n - 1)
                nc.scalar.activation(q_out[0:TB, t, 0:C], q_full[0:TB, t], ACT.Copy).then_inc(s_qhi, 1)
                act.wait_ge(s_qr1, n + 1)
                nc.scalar.activation(q_out[0:TB, t, C:2 * C], q_rest[0:TB, t, 0], ACT.Copy).then_inc(s_qmid, 1)
                act.wait_ge(s_qr2, n + 1)
                nc.scalar.activation(q_out[0:TB, t, 2 * C:3 * C], q_rest[0:TB, t, 1], ACT.Copy)\
                    .then_inc(s_qlo, 1)

            for t in range(2):
                parts(t, 0)
            with act.Fori(1, NODE_TILES // 2) as turn:
                for t in range(2):
                    parts(t, turn)

            def copy_onehotT(n, slot):
                act.wait_ge(s_ohT, n + 1)
                if exists(n - 2, BATCHES):
                    act.wait_ge(s_qe, n - 1)
                nc.scalar.activation(onehotT[:, slot % 2], bank[slot % 2][:], ACT.Copy).then_inc(s_ohTc, 1)

            def exponent(n, slot):
                act.wait_ge(s_clip, n + 1)
                if exists(n - 3, BATCHES):
                    act.wait_ge(s_acc, n - 2)
                nc.scalar.activation(ev[:, slot % BATCHES_PER_GROUP, :, C:ACC],
                                     clipped[:, slot % 2].rearrange("p (i h) -> p i h", h=H),
                                     ACT.Exp, scale=SCALE).then_inc(s_exp, 1)

            def finish_group(g, t):
                act.wait_ge(s_grp, g + 1)
                if exists(g - 2, GROUPS):
                    act.wait_ge(s_aggst, 16 * (g - 1))
                nc.scalar.activation(acc_sb[:, t], bank[2 + t][:, 0:ACC], ACT.Copy).then_inc(s_accc, 1)
                base = act.value_load(bases_sb[0:1, bass.ds(g, 1)], min_val=0, max_val=NODES - 1)
                act.wait_ge(s_accc, g + 1)
                if exists(g - 1, GROUPS):
                    act.wait_ge(s_aggst, 16 * g)
                act.dma_start(agg_dram[bass.ds(base, P), :], acc_sb[:, t]).then_inc(s_aggst, 16)

            def edges(turn):
                for slot in range(SLOTS):
                    n = SLOTS * turn + slot
                    t, b = divmod(slot, BATCHES_PER_GROUP)
                    if exists(n + 1, BATCHES):
                        copy_onehotT(n + 1, (slot + 1) % SLOTS)
                    exponent(n, slot)
                    g = 2 * turn + t - 1
                    if b == BATCHES_PER_GROUP - 1 and exists(g, GROUPS):
                        finish_group(g, 1 - t)

            act.wait_ge(s_const, 6)
            act.wait_ge(s_zero, 32)
            copy_onehotT(0, 0)
            turns(act, edges, TURNS)
            finish_group(GROUPS - 1, (GROUPS - 1) % 2)

            act.wait_ge(s_w3, 16 * 7)

            def copy_wvT(s, t):
                act.wait_ge(s3_wvT, s + 1)
                if exists(s - 1, SUPERBLOCKS):
                    act.wait_ge(s3_y, s)
                nc.scalar.activation(wvT[:].rearrange("p a k n -> p (a k n)"),
                                     bank[0][:, 0:SB_TILES * C * TB // P], ACT.Copy).then_inc(s3_wvTc, 1)

            def copy_hT(s, t):
                act.wait_ge(s3_hTp, s + 1)
                if exists(s - 1, SUPERBLOCKS):
                    act.wait_ge(s3_f1, (FC // 2) * s)
                for k in range(KC):
                    last = nc.scalar.activation(hT[:, k], bank[2][:, k * SB:(k + 1) * SB], ACT.Identity,
                                                scale=lngb_sb[:, k, 0:1], bias=lngb_sb[:, k, 1:2])
                last.then_inc(s3_hT, 1)

            def gelu(s, t):
                for pair in range(FC // 2):
                    act.wait_ge(s3_f1, (FC // 2) * s + pair + 1)
                    if pair == 0 and exists(s - 1, SUPERBLOCKS):
                        act.wait_ge(s3_f2, 2 * s)
                    for j in range(2):
                        f = 2 * pair + j
                        last = nc.scalar.activation(hidT[:, f], quad[:, pair % 2, j * SB:(j + 1) * SB],
                                                    ACT.Gelu, bias=b1_sb[:, f:f + 1])
                    last.then_inc(s3_gelu, 1)

            def superblock(s, t):
                gelu(s, t)
                if exists(s + 1, SUPERBLOCKS):
                    copy_wvT(s + 1, 1 - t)
                    copy_hT(s + 1, 1 - t)

            copy_wvT(0, 0)
            copy_hT(0, 0)
            superblock(0, 0)
            superblock(1, 1)
            with act.Fori(1, SUPERBLOCKS // 2) as turn:
                for t in range(2):
                    superblock(2 * turn + t, t)
            superblock(SUPERBLOCKS - 1, 0)

        @block.vector
        def _(dve):
            def biases(t, turn):
                n = 2 * turn + t
                dve.wait_ge(s_mm, n + 1)
                if exists(turn - 1, NODE_TILES // 2):
                    dve.wait_ge(s_qr1, n - 1)
                nc.vector.tensor_tensor(q_full[0:TB, t], bank[2 + t][0:TB, 0:C], bqkv_sb[0:TB, 0:C],
                                        ALU.add).then_inc(s_qfull, 1)
                if exists(turn - 1, NODE_TILES // 2):
                    dve.wait_ge(s_kvst[t], 16 * turn)
                nc.vector.tensor_tensor(kv_out[0:TB, t], quad[0:TB, t, :], bqkv_sb[0:TB, C:3 * C],
                                        ALU.add).then_inc(s_kvb, 1)

            dve.wait_ge(s_w, 32)
            for t in range(2):
                biases(t, 0)
            with dve.Fori(1, NODE_TILES // 2) as turn:
                for t in range(2):
                    biases(t, turn)

            def locate(g, t, turn):
                dve.wait_ge(s_dst[t], 16 * (turn + 1))
                if exists(g - 2, GROUPS):
                    dve.wait_ge(s_oh, BATCHES_PER_GROUP * (g - 1))
                    dve.wait_ge(s_csel, g - 1)
                nc.vector.tensor_tensor(dloc[:, t], dst_sb[:, t],
                                        dst_sb[:, t, TPG:TPG + 1].broadcast_to([P, TPG + 2]),
                                        ALU.subtract).then_inc(s_dloc, 1)

            def select_carry(g, t):
                if exists(g - 2, GROUPS):
                    dve.wait_ge(s_grp, g - 1)
                dve.wait_ge(s_dloc, g + 1)
                nc.vector.tensor_scalar(carry_sel[:, t, 0:1], iota_col[:], dloc[:, t, TPG + 1:TPG + 2], 0.0,
                                        ALU.add, ALU.is_equal).then_inc(s_csel, 1)

            def onehots(n, slot, g, turn):
                t, b = divmod(slot, BATCHES_PER_GROUP)
                if b == 0:
                    locate(g, t, turn)
                    select_carry(g, t)
                if exists(n - SLOTS, BATCHES):
                    dve.wait_ge(s_acc, n - SLOTS + 1)
                cols = dloc[:, t, b * TILES_PER_BATCH:(b + 1) * TILES_PER_BATCH]
                nc.vector.tensor_tensor(onehot[:, slot],
                                        iota_row[:].unsqueeze(1).broadcast_to([P, TILES_PER_BATCH, P]),
                                        cols.unsqueeze(2).broadcast_to([P, TILES_PER_BATCH, P]),
                                        ALU.is_equal).then_inc(s_oh, 1)

            def products(n, slot, turn):
                dve.wait_ge(s_kv[slot], 64 * (turn + 1))
                dve.wait_ge(s_qe, n + 1)
                if exists(n - 2, BATCHES):
                    dve.wait_ge(s_score, n - 1)
                h = slot % 2
                nc.vector.tensor_tensor(prod[:, h].rearrange("p (i c) -> p i c", c=C), kv[:, slot, :, 0:C],
                                        quad[:, 2 * h:2 * h + 2, :].rearrange("p a (b c) -> p (a b) c", c=C),
                                        ALU.mult).then_inc(s_prod, 1)

            def scores(n, slot):
                dve.wait_ge(s_prod, n + 1)
                if exists(n - 2, BATCHES):
                    dve.wait_ge(s_clip, n - 1)
                nc.vector.tensor_reduce(score[:, slot % 2], prod[:, slot % 2].rearrange("p (h d) -> p h d", d=HD),
                                        AX.X, ALU.add).then_inc(s_score, 1)

            def clip(n, slot):
                dve.wait_ge(s_score, n + 1)
                if exists(n - 2, BATCHES):
                    dve.wait_ge(s_exp, n - 1)
                nc.vector.tensor_scalar(clipped[:, slot % 2], score[:, slot % 2], CLIP / SCALE, -CLIP / SCALE,
                                        ALU.min, ALU.max).then_inc(s_clip, 1)

            def weight(n, slot, turn):
                dve.wait_ge(s_exp, n + 1)
                b = slot % BATCHES_PER_GROUP
                shape = [P, TILES_PER_BATCH, H, HD]
                nc.vector.tensor_tensor(ev[:, b, :, 0:C].rearrange("p i (h d) -> p i h d", d=HD),
                                        kv[:, slot, :, C:2 * C].rearrange("p i (h d) -> p i h d", d=HD),
                                        ev[:, b, :, C:ACC].unsqueeze(3).broadcast_to(shape),
                                        ALU.mult).then_inc(s_ev, 1)

            def edges(turn):
                for slot in range(SLOTS):
                    n = SLOTS * turn + slot
                    products(n, slot, turn)
                    if exists(n - 1, BATCHES):
                        weight(n - 1, (slot - 1) % SLOTS, turn)
                    scores(n, slot)
                    if exists(n + 2, BATCHES):
                        ahead = (slot + 2) % SLOTS
                        onehots(n + 2, ahead, 2 * turn + (slot + 2) // BATCHES_PER_GROUP,
                                turn + (slot + 2) // SLOTS)
                    clip(n, slot)

            dve.wait_ge(s_const, 6)
            onehots(0, 0, 0, 0)
            onehots(1, 1, 0, 0)
            turns(dve, edges, TURNS)
            weight(BATCHES - 1, SLOTS - 1, TURNS - 1)

            def normalise(s, t, turn):
                dve.wait_ge(s3_in[t], 32 * (turn + 1))
                if exists(s - 2, SUPERBLOCKS):
                    dve.wait_ge(s3_rden, s - 1)
                nc.vector.tensor_scalar(den[0:TB, t], agg_in[0:TB, t, :, C:ACC], 1e-30, None, ALU.max)\
                    .then_inc(s3_den, 1)
                dve.wait_ge(s3_den, s + 1)
                if exists(s - 1, SUPERBLOCKS):
                    dve.wait_ge(s3_wv, s)
                nc.vector.reciprocal(rden[0:TB, t], den[0:TB, t]).then_inc(s3_rden, 1)
                dve.wait_ge(s3_rden, s + 1)
                if exists(s - 1, SUPERBLOCKS):
                    dve.wait_ge(s3_wvT, s)
                nc.vector.tensor_tensor(wv[0:TB].rearrange("p a (h d) -> p a h d", d=HD),
                                        agg_in[0:TB, t, :, 0:C].rearrange("p a (h d) -> p a h d", d=HD),
                                        rden[0:TB, t].unsqueeze(3).broadcast_to([TB, SB_TILES, H, HD]),
                                        ALU.mult).then_inc(s3_wv, 1)

            def residual(s, t):
                dve.wait_ge(s3_y, s + 1)
                dve.wait_ge(s3_xbp, s + 1)
                if exists(s - 2, SUPERBLOCKS):
                    dve.wait_ge(s3_xx, s - 1)
                nc.vector.tensor_tensor(x2[0:TB, t], bank[1][0:TB, 0:SB_TILES * C]
                                        .rearrange("p (a c) -> p a c", c=C), x_bp[0:TB, t],
                                        ALU.add).then_inc(s3_x2, 1)

            def inverse_root(s, var, r, s_rs):
                v, half, shifted, y, y2 = (r[0:TB, :, c:c + 1] for c in (1, 2, 3, 0, 4))
                steps = [0]

                def step(instruction):
                    instruction.then_inc(s_rs, 1)
                    steps[0] += 1
                    dve.wait_ge(s_rs, ROOT_STEPS * s + steps[0])

                step(nc.vector.tensor_scalar(v, var, EPS, None, ALU.add))
                nc.vector.tensor_scalar(half, v, -0.5, None, ALU.mult).then_inc(s_rs, 1)
                steps[0] += 1
                step(nc.vector.tensor_scalar(shifted.bitcast(i32), v.bitcast(i32), 1, None,
                                             ALU.logical_shift_right))
                step(nc.vector.tensor_scalar(y.bitcast(i32), shifted.bitcast(i32), -1.0, ROOT_MAGIC,
                                             ALU.mult, ALU.add))
                for _ in range(NEWTON):
                    step(nc.vector.tensor_tensor(y2, y, y, ALU.mult))
                    step(nc.vector.tensor_tensor(y2, y2, half, ALU.mult))
                    step(nc.vector.scalar_tensor_tensor(y, y2, 1.5, y, ALU.add, ALU.mult))
                assert steps[0] == ROOT_STEPS

            def layer_norm(s, src, dst, st, mvt, rs, s_in, s_st, s_mv, s_rs, s_out):
                dve.wait_ge(s_in, s + 1)
                if exists(s - 1, SUPERBLOCKS):
                    dve.wait_ge(s_mv, s)
                    dve.wait_ge(s_out, s)
                for a in range(SB_TILES):
                    last = nc.vector.bn_stats(st[0:TB, a], src[0:TB, a])
                last.then_inc(s_st, 1)
                dve.wait_ge(s_st, s + 1)
                dve.sem_inc(s_gate_dve, 1)
                for a in range(SB_TILES):
                    last = nc.vector.bn_aggr(mvt[0:TB, a], st[0:TB, a])
                last.then_inc(s_mv, 1)
                dve.wait_ge(s_mv, s + 1)
                inverse_root(s, mvt[0:TB, :, 1:2], rs, s_rs)
                for a in range(SB_TILES):
                    last = nc.vector.tensor_scalar(dst[0:TB, a], src[0:TB, a], mvt[0:TB, a, 0:1], rs[0:TB, a, 0:1],
                                                   ALU.subtract, ALU.mult)
                last.then_inc(s_out, 1)

            def front_norm(s, t):
                if exists(s - 1, SUPERBLOCKS):
                    dve.wait_ge(s3_hTp, s)
                layer_norm(s, x2[:, t], hn, stats, mv, rstd, s3_x2, s3_st, s3_mv, s3_rs, s3_hn)

            def finish(s, t, turn):
                dve.wait_ge(s3_f2, 2 * (s + 1))
                dve.wait_ge(s3_xx, s + 1)
                if exists(s - 1, SUPERBLOCKS):
                    dve.wait_ge(s3_out, s)
                nc.vector.tensor_tensor(z[0:TB], quad[0:TB, 2 + t, :].rearrange("p (a c) -> p a c", c=C),
                                        xx[0:TB, t], ALU.add).then_inc(s3_z, 1)
                if exists(s - 2, SUPERBLOCKS):
                    dve.wait_ge(s3_st_out[t], 16 * turn)
                layer_norm(s, z, y_out[:, t], zstats, zmv, zrstd, s3_z, s3_zst, s3_zmv, s3_zrs, s3_out)

            def superblock(s, t, turn):
                if exists(s + 1, SUPERBLOCKS):
                    normalise(s + 1, 1 - t, turn + t)
                    residual(s + 1, 1 - t)
                    front_norm(s + 1, 1 - t)
                finish(s, t, turn)

            normalise(0, 0, 0)
            residual(0, 0)
            front_norm(0, 0)
            superblock(0, 0, 0)
            superblock(1, 1, 0)
            with dve.Fori(1, SUPERBLOCKS // 2) as turn:
                for t in range(2):
                    superblock(2 * turn + t, t, turn)
            superblock(SUPERBLOCKS - 1, 0, SUPERBLOCKS // 2)


def kernel(**inputs):
    import numpy as np
    import concourse.bacc as bacc
    from concourse.bass_utils import run_bass_kernel_spmd

    p = "L0_gnn_"
    a = {k: np.asarray(v) for k, v in inputs.items()}
    x = a["x"]
    fill = GROUPS * TPG * P - EDGES
    src = np.concatenate([a["src"], np.zeros(fill, a["src"].dtype)])
    dst = np.concatenate([a["dst"], np.full(fill, NO_NODE, a["dst"].dtype)])

    def by_group(e):
        return np.ascontiguousarray(e.reshape(GROUPS, TPG, P).transpose(0, 2, 1))

    first = np.minimum(np.arange(GROUPS) * TPG * P, (EDGES - 1) // (TPG * P) * TPG * P)
    bases = np.concatenate([np.zeros(1, dst.dtype), dst[first[1:]]])
    before = np.concatenate([np.full(1, -NO_NODE, dst.dtype), bases[:-1]])
    columns = np.stack([bases, before], axis=1)
    edge_dst = np.concatenate([by_group(dst), np.broadcast_to(columns[:, None, :], (GROUPS, P, 2))], axis=2)
    arrays = {
        "xT": x.T, "x": x,
        "w_qkvT": np.concatenate([a[p + "Wq"], a[p + "Wk"], a[p + "Wv"]], axis=0).T,
        "b_qkv": np.concatenate([a[p + "bq"], a[p + "bk"], a[p + "bv"]])[None],
        "wpT": a[p + "Wp"].T, "bp": a[p + "bp"][None],
        "ln_gb": np.stack([a[p + "ln_g"], a[p + "ln_b"]], axis=1).reshape(KC, P, 2).transpose(1, 0, 2),
        "w1T": a[p + "W1"].T, "b1": a[p + "b1"].reshape(FC, P).T,
        "w2T": a[p + "W2"].T, "b2": a[p + "b2"][None],
        "edge_src": by_group(src), "edge_dst": edge_dst, "bases": bases[None],
    }
    nc = bacc.Bacc("TRN2", target_bir_lowering=False, num_devices=1)
    args = []
    arrays = {k: np.ascontiguousarray(v) for k, v in arrays.items()}
    for name, v in arrays.items():
        args.append(nc.dram_tensor(name, v.shape, mybir.dt.from_np(v.dtype), kind="ExternalInput").ap())
    args.append(nc.dram_tensor("out", (NODES, C), mybir.dt.float32, kind="ExternalOutput").ap())
    gnn_program(nc, *args)
    r = run_bass_kernel_spmd(nc, [arrays], core_ids=[0])
    return r.results[0]["out"]
```

```python
import concourse.bass as bass
from concourse import mybir
from contextlib import ExitStack

P = 128
NODES, EDGES, C, H = 6250, 100000, 256, 8
HD = C // H
HIDDEN = 4 * C
TILES_PER_BATCH = 4
BATCHES_PER_GROUP = 3
X_SLOTS = 4
TPG = TILES_PER_BATCH * BATCHES_PER_GROUP
EDGE_TILES = -(-EDGES // P)
GROUPS = -(-EDGE_TILES // TPG)
GROUPS += GROUPS % 2
BATCHES = GROUPS * BATCHES_PER_GROUP
SLOTS = 2 * BATCHES_PER_GROUP
TURNS = GROUPS // 2
AHEAD = BATCHES_PER_GROUP
ACC = C + H
XCOLS = 125
TB = 125
NODE_TILES = NODES // TB
SB_TILES = 2
SB = TB * SB_TILES
SUPERBLOCKS = NODE_TILES // SB_TILES
KC = C // P
FC = HIDDEN // P
CLIP = 10.0
SCALE = float(HD) ** -0.5
EPS = 1e-5
NEWTON = 3
NORM_STEPS = 5 + 3 * NEWTON
ROOT_MAGIC = float(0x5F3759DF)
NO_NODE = 1 << 20


def gnn_program(nc, xT, x, w_qkvT, b_qkv, wpT, bp, ln_gb, w1T, b1, w2T, b2, edge_src, edge_dst, bases, out):
    f32, f32r, i32 = mybir.dt.float32, mybir.dt.float32r, mybir.dt.int32
    ALU, ACT, AX = mybir.AluOpType, mybir.ActivationFunctionType, mybir.AxisListType

    kv_dram = nc.dram_tensor("kv_rows", [NODES, 2 * C], f32).ap()
    q_dram = nc.dram_tensor("q_parts", [NODES + P, 2 * C], f32).ap()
    agg_dram = nc.dram_tensor("agg_rows", [NODES + P, ACC], f32).ap()

    ctx, early = ExitStack(), ExitStack()
    with ctx:
        def sb(name, shape, dt=f32, stack=ctx):
            return stack.enter_context(nc.sbuf_tensor(name, shape, dt))

        def sem(name):
            return ctx.enter_context(nc.semaphore(name))

        iota_row = sb("iota_row", [P, P])
        iota_col = sb("iota_col", [P, 1])
        ident = sb("ident", [P, P])
        wp_sb = sb("wp_sb", [P, 2, KC * C], f32r)
        w1_sb = sb("w1_sb", [P, 2, KC * HIDDEN], f32r)
        w2_sb = sb("w2_sb", [P, 2, FC * C], f32r)
        bp_sb = sb("bp_sb", [P, C])
        b2_sb = sb("b2_sb", [P, C])
        lngb_sb = sb("lngb_sb", [P, KC, 2])
        b1_sb = sb("b1_sb", [P, FC])
        bases_sb = sb("bases_sb", [1, GROUPS], i32)
        zeros = sb("zeros", [P, 2 * C], f32, early)
        wqkv_in = sb("wqkv_in", [P, KC * 3 * C], f32, early)
        wp_in = sb("wp_in", [P, KC * C], f32, early)
        w1_in = sb("w1_in", [P, KC * HIDDEN], f32, early)
        w2_in = sb("w2_in", [P, FC * C], f32, early)
        wqkv_sb = sb("wqkv_sb", [P, 2, KC * 3 * C], f32r, early)
        bqkv_sb = sb("bqkv_sb", [P, 3 * C], f32, early)
        xT_sb = sb("xT_sb", [P, X_SLOTS, KC, XCOLS], f32, early)
        xT_parts = sb("xT_parts", [P, 2, 2, KC, XCOLS], f32r, early)
        q_full = sb("q_full", [P, 2, C], f32, early)
        q_out = sb("q_out", [P, 2, 2, C], f32r, early)
        kv_out = sb("kv_out", [P, 2, 2 * C], f32, early)
        src_sb = sb("src_sb", [P, 2, TPG], i32, early)
        dst_sb = sb("dst_sb", [P, 2, TPG + 2], i32, early)
        dloc = sb("dloc", [P, 2, TPG + 2], f32, early)
        qwin = sb("qwin", [P, 2, 2 * C], f32r, early)
        kv = sb("kv", [P, SLOTS, TILES_PER_BATCH, 2 * C], f32, early)
        onehot = sb("onehot", [P, SLOTS, TILES_PER_BATCH, P], f32, early)
        onehotT = sb("onehotT", [P, 2, TILES_PER_BATCH * P], f32r, early)
        prod = sb("prod", [P, 2, TILES_PER_BATCH * C], f32, early)
        score = sb("score", [P, 2, TILES_PER_BATCH * H], f32, early)
        clipped = sb("clipped", [P, 2, TILES_PER_BATCH * H], f32, early)
        ev = sb("ev", [P, BATCHES_PER_GROUP, TILES_PER_BATCH, ACC], f32, early)
        carry_sel = sb("carry_sel", [P, 2, P], f32, early)
        acc_sb = sb("acc_sb", [P, 2, ACC], f32, early)
        early.close()
        agg_in = sb("agg_in", [P, 2, SB_TILES, ACC])
        x_in = sb("x_in", [P, 2, SB_TILES, C])
        den = sb("den", [P, SB_TILES, H])
        rden = sb("rden", [P, SB_TILES, H])
        wv = sb("wv", [P, SB_TILES, C])
        wvT = sb("wvT", [P, 2, SB_TILES * KC * XCOLS], f32r)
        x_bp = sb("x_bp", [P, 2, SB_TILES, C])
        x_b2 = sb("x_b2", [P, 2, SB_TILES, C])
        x2 = sb("x2", [P, 2, SB_TILES, C])
        xx = sb("xx", [P, 2, SB_TILES, C])
        hn = sb("hn", [P, SB_TILES, C])
        hT_full = sb("hT_full", [P, KC * SB])
        hT = sb("hT", [P, 2, KC * SB], f32r)
        hid_full = sb("hid_full", [P, FC, SB])
        hid = sb("hid", [P, 2, FC, SB], f32r)
        z = sb("z", [P, SB_TILES, C])
        y_out = sb("y_out", [P, 2, SB_TILES, C])
        stats = sb("stats", [P, 2 * SB_TILES, 6])
        mv = sb("mv", [P, 2 * SB_TILES, 2])
        root = sb("root", [P, 2 * SB_TILES, 5])

        bank = [ctx.enter_context(nc.psum_tensor(f"bank{i}", [P, 512], f32)) for i in range(4)]
        quad = ctx.enter_context(nc.psum_tensor("quad", [P, 4, 512], f32))

        s_w = sem("weights_in")
        s_w3 = sem("weights3_in")
        s_id = sem("ident_steps")
        s_const = sem("constants_ready")
        s_zero = sem("tails_zeroed")
        s_wqkv = sem("wqkv_parts")
        s_wparts = sem("weight_parts")
        s_xhi = sem("xT_hi_done")
        s_xlo = sem("xT_lo_done")
        s_x = [sem(f"xT_in{t}") for t in range(X_SLOTS)]
        s_mm = sem("qkv_done")
        s_qfull = sem("q_biased")
        s_qhi = sem("q_hi_done")
        s_qlo = sem("q_lo_done")
        s_kvb = sem("kv_biased")
        s_qst = [sem(f"q_stored{t}") for t in range(2)]
        s_kvst = [sem(f"kv_stored{t}") for t in range(2)]
        s_src = [sem(f"src_in{t}") for t in range(2)]
        s_dst = [sem(f"dst_in{t}") for t in range(2)]
        s_qwin = [sem(f"qwin_in{t}") for t in range(2)]
        s_kv = [sem(f"kv_in{t}") for t in range(SLOTS)]
        s_dloc = sem("dloc_ready")
        s_csel = sem("carry_sel_ready")
        s_oh = sem("onehot_ready")
        s_ohT = sem("onehot_transposed")
        s_ohTc = sem("onehotT_copied")
        s_qe = sem("q_rows_ready")
        s_prod = sem("prod_ready")
        s_score = sem("score_ready")
        s_clip = sem("clipped_ready")
        s_exp = sem("exp_ready")
        s_ev = sem("weighted_ready")
        s_acc = sem("batch_summed")
        s_grp = sem("group_summed")
        s_accc = sem("sums_copied")
        s_aggst = sem("sums_stored")
        s3_in = [sem(f"node_rows_in{t}") for t in range(2)]
        s3_den = sem("den_guarded")
        s3_rden = sem("den_inverted")
        s3_wv = sem("wv_ready")
        s3_wvT = sem("wv_transposed")
        s3_wvThi = sem("wvT_hi_done")
        s3_wvTlo = sem("wvT_lo_done")
        s3_xbp = sem("x_bp_ready")
        s3_xb2 = sem("x_b2_ready")
        s3_y = sem("projected")
        s3_x2 = sem("x2_ready")
        s3_xx = sem("xx_ready")
        s3_z = sem("z_ready")
        s3_ln = sem("norm_steps")
        s3_hn = sem("hn_ready")
        s3_hTp = sem("h_transposed")
        s3_hTf = sem("hT_full_done")
        s3_hThi = sem("hT_hi_done")
        s3_hTlo = sem("hT_lo_done")
        s3_f1 = sem("ffn1_done")
        s3_gelu = sem("gelu_done")
        s3_hidhi = sem("hid_hi_done")
        s3_hidlo = sem("hid_lo_done")
        s3_f2 = sem("ffn2_done")
        s3_out = sem("y_out_ready")
        s3_st_out = [sem(f"out_stored{t}") for t in range(2)]

        block = ctx.enter_context(nc.Block())

        s_gate_pool = sem("gate_pool")
        s_gate_dve = sem("gate_dve")

        def turns(eng, body, count):
            body(0)
            with eng.Fori(1, count - 1) as turn:
                body(turn)
            body(count - 1)

        def walk_tiles(eng, body):
            def four(turn):
                for i in range(X_SLOTS):
                    if exists(X_SLOTS * turn + i, NODE_TILES):
                        body(X_SLOTS * turn + i, i, turn, i % 2, 2 * turn + i // 2)

            four(0)
            with eng.Fori(1, NODE_TILES // X_SLOTS) as turn:
                four(turn)
            four(NODE_TILES // X_SLOTS)

        def exists(n, count):
            return 0 <= n < count if isinstance(n, int) else True

        @block.sync
        def _(sp):
            sp.dma_start(wqkv_in[:].rearrange("p (k n) -> p k n", k=KC),
                         w_qkvT.rearrange("(k p) n -> p k n", p=P)).then_inc(s_w, 16)
            sp.dma_start(bqkv_sb[:], b_qkv.broadcast_to([P, 3 * C])).then_inc(s_w, 16)

            def load_x(n, slot):
                if exists(n - X_SLOTS, NODE_TILES):
                    sp.wait_ge(s_xlo, n - X_SLOTS + 1)
                sp.dma_start(xT_sb[:, slot], xT[:, bass.ds(n * TB, TB)].rearrange("(k p) n -> p k n", p=P))\
                    .then_inc(s_x[slot], 16)

            def move_rows(n, slot, turn, t, uses):
                row = n * TB
                sp.wait_ge(s_qlo, n + 1)
                sp.dma_start(q_dram[bass.ds(row, TB), :],
                             q_out[0:TB, t].rearrange("p a c -> p (a c)").bitcast(f32)).then_inc(s_qst[t], 16)
                sp.wait_ge(s_kvb, n + 1)
                sp.dma_start(kv_dram[bass.ds(row, TB), :], kv_out[0:TB, t]).then_inc(s_kvst[t], 16)
                if exists(n + X_SLOTS, NODE_TILES):
                    load_x(n + X_SLOTS, slot)

            n1 = NODE_TILES // 2
            for slot in range(X_SLOTS):
                load_x(slot, slot)
            for w, wT, k in ((wp_in, wpT, KC), (w1_in, w1T, KC), (w2_in, w2T, FC)):
                sp.dma_start(w[:].rearrange("p (k n) -> p k n", k=k),
                             wT.rearrange("(k p) n -> p k n", p=P)).then_inc(s_w3, 16)
            sp.dma_start(bp_sb[:], bp.broadcast_to([P, C])).then_inc(s_w3, 16)
            sp.dma_start(b2_sb[:], b2.broadcast_to([P, C])).then_inc(s_w3, 16)
            sp.dma_start(lngb_sb[:], ln_gb).then_inc(s_w3, 16)
            sp.dma_start(b1_sb[:], b1).then_inc(s_w3, 16)
            for n in range(X_SLOTS):
                move_rows(n, n, 0, n % 2, n // 2)
            with sp.Fori(1, NODE_TILES // X_SLOTS - 1) as turn:
                for i in range(X_SLOTS):
                    move_rows(X_SLOTS * turn + i, i, turn, i % 2, 2 * turn + i // 2)
            for n in range(NODE_TILES // X_SLOTS * X_SLOTS - X_SLOTS, NODE_TILES):
                move_rows(n, n % X_SLOTS, n // X_SLOTS, n % 2, n // 2)
            sp.wait_ge(s_const, 1)
            sp.dma_start(q_dram[NODES:NODES + P, :], zeros[:]).then_inc(s_zero, 16)
            sp.dma_start(bases_sb[:], bases).then_inc(s_zero, 16)

            sp.wait_ge(s_zero, 32)
            for t in range(2):
                sp.wait_ge(s_qst[t], 16 * n1)

            def load_group(g, t, turn):
                if exists(turn - 1, TURNS):
                    for b in range(BATCHES_PER_GROUP):
                        sp.wait_ge(s_kv[t * BATCHES_PER_GROUP + b], 64 * turn)
                sp.dma_start(src_sb[:, t], edge_src[bass.ds(g, 1), :, :].rearrange("g p n -> (g p) n"))\
                    .then_inc(s_src[t], 16)
                if exists(turn - 1, TURNS):
                    sp.wait_ge(s_dloc, g - 1)
                sp.dma_start(dst_sb[:, t], edge_dst[bass.ds(g, 1), :, :].rearrange("g p n -> (g p) n"))\
                    .then_inc(s_dst[t], 16)
                base = sp.value_load(bases_sb[0:1, bass.ds(g, 1)], min_val=0, max_val=NODES - 1)
                if exists(turn - 1, TURNS):
                    sp.wait_ge(s_qe, BATCHES_PER_GROUP * (g - 1))
                sp.dma_start(qwin[:, t].bitcast(f32), q_dram[bass.ds(base, P), :]).then_inc(s_qwin[t], 16)

            load_group(0, 0, 0)
            load_group(1, 1, 0)
            with sp.Fori(1, TURNS) as turn:
                for t in range(2):
                    load_group(2 * turn + t, t, turn)

            sp.wait_ge(s_aggst, 16 * GROUPS)

            def load_nodes(s, t):
                if exists(s - 2, SUPERBLOCKS):
                    sp.wait_ge(s3_wv, s - 1)
                    sp.wait_ge(s3_xb2, s - 1)
                rows = bass.ds(s * SB, SB)
                sp.dma_start(agg_in[0:TB, t], agg_dram[rows, :].rearrange("(a p) n -> p a n", p=TB))\
                    .then_inc(s3_in[t], 16)
                sp.dma_start(x_in[0:TB, t], x[rows, :].rearrange("(a p) n -> p a n", p=TB))\
                    .then_inc(s3_in[t], 16)

            def store_nodes(s, t):
                sp.wait_ge(s3_out, s + 1)
                sp.dma_start(out[bass.ds(s * SB, SB), :].rearrange("(a p) n -> p a n", p=TB),
                             y_out[0:TB, t]).then_inc(s3_st_out[t], 16)

            for s in range(4):
                load_nodes(s, s % 2)
            store_nodes(0, 0)
            load_nodes(4, 0)
            store_nodes(1, 1)
            load_nodes(5, 1)
            with sp.Fori(3, SUPERBLOCKS // 2) as turn:
                for t in range(2):
                    store_nodes(2 * turn + t - 4, t)
                    load_nodes(2 * turn + t, t)
            for s in range(SUPERBLOCKS - 1, SUPERBLOCKS + 4):
                store_nodes(s - 4, s % 2)
                if s < SUPERBLOCKS:
                    load_nodes(s, s % 2)
            sp.wait_ge(s3_st_out[0], 16 * (SUPERBLOCKS // 2 + 1))
            sp.wait_ge(s3_st_out[1], 16 * (SUPERBLOCKS // 2))

        @block.gpsimd
        def _(pool):
            nc.gpsimd.memset(zeros[:], 0.0).then_inc(s_const, 1)
            nc.gpsimd.iota(iota_row[:], [[1, P]], base=0, channel_multiplier=0,
                           allow_small_or_imprecise_dtypes=True).then_inc(s_const, 1)
            nc.gpsimd.iota(iota_col[:], [[0, 1]], base=0, channel_multiplier=1,
                           allow_small_or_imprecise_dtypes=True).then_inc(s_const, 1)
            nc.gpsimd.memset(ident[:], 0.0).then_inc(s_id, 1)
            nc.gpsimd.memset(carry_sel[:], 0.0).then_inc(s_const, 1)
            nc.gpsimd.memset(acc_sb[:], 0.0).then_inc(s_const, 1)
            pool.wait_ge(s_id, 1)
            nc.gpsimd.affine_select(out=ident[:], in_=ident[:], compare_op=ALU.not_equal, fill=1.0,
                                    base=0, pattern=[[-1, P]], channel_multiplier=1).then_inc(s_const, 1)

            def q_low(n, slot, turn, t, uses):
                pool.wait_ge(s_qhi, n + 1)
                if exists(n - 2, NODE_TILES):
                    pool.wait_ge(s_qst[t], 16 * uses)
                nc.gpsimd.tensor_tensor(q_out[0:TB, t, 1], q_full[0:TB, t], q_out[0:TB, t, 0].bitcast(f32),
                                        ALU.subtract).then_inc(s_qlo, 1)

            walk_tiles(pool, q_low)

            for t in range(2):
                pool.wait_ge(s_kvst[t], 16 * (NODE_TILES // 2))

            def gather(turn):
                for slot in range(SLOTS):
                    t, b = divmod(slot, BATCHES_PER_GROUP)
                    if b == 0:
                        pool.wait_ge(s_src[t], 16 * (turn + 1))
                    if exists(turn - 1, TURNS):
                        pool.wait_ge(s_ev, SLOTS * turn + slot - SLOTS + 1)
                    pool.sem_inc(s_gate_pool, 1)
                    for i in range(TILES_PER_BATCH):
                        col = b * TILES_PER_BATCH + i
                        nc.gpsimd.indirect_dma_start(
                            out=kv[:, slot, i, :], out_offset=None, in_=kv_dram,
                            in_offset=bass.IndirectOffsetOnAxis(ap=src_sb[:, t, col:col + 1], axis=0),
                        ).then_inc(s_kv[slot], 16)

            turns(pool, gather, TURNS)

            def x_sums(s, t, turn):
                pool.wait_ge(s3_in[t], 32 * (turn + 1))
                if exists(s - 2, SUPERBLOCKS):
                    pool.wait_ge(s3_x2, s - 1)
                for a in range(SB_TILES):
                    last = nc.gpsimd.tensor_tensor(x_bp[0:TB, t, a], x_in[0:TB, t, a], bp_sb[0:TB], ALU.add)
                last.then_inc(s3_xbp, 1)
                if exists(s - 2, SUPERBLOCKS):
                    pool.wait_ge(s3_xx, s - 1)
                for a in range(SB_TILES):
                    last = nc.gpsimd.tensor_tensor(x_b2[0:TB, t, a], x_in[0:TB, t, a], b2_sb[0:TB], ALU.add)
                last.then_inc(s3_xb2, 1)

            def residuals(s, t):
                pool.wait_ge(s3_x2, s + 1)
                pool.wait_ge(s3_xb2, s + 1)
                if exists(s - 2, SUPERBLOCKS):
                    pool.wait_ge(s3_z, s - 1)
                nc.gpsimd.tensor_tensor(xx[0:TB, t], x2[0:TB, t], x_b2[0:TB, t], ALU.add).then_inc(s3_xx, 1)

            def h_low(s):
                pool.wait_ge(s3_hThi, s + 1)
                if exists(s - 1, SUPERBLOCKS):
                    pool.wait_ge(s3_f1, (FC // 2) * s)
                nc.gpsimd.tensor_tensor(hT[:, 1], hT_full[:], hT[:, 0].bitcast(f32), ALU.subtract)\
                    .then_inc(s3_hTlo, 1)

            def hid_low(s):
                for pair in range(FC // 2):
                    pool.wait_ge(s3_hidhi, (FC // 2) * s + pair + 1)
                    if pair == 0 and exists(s - 1, SUPERBLOCKS):
                        pool.wait_ge(s3_f2, 2 * s)
                    fs = slice(2 * pair, 2 * pair + 2)
                    nc.gpsimd.tensor_tensor(hid[:, 1, fs], hid_full[:, fs], hid[:, 0, fs].bitcast(f32),
                                            ALU.subtract).then_inc(s3_hidlo, 1)

            def superblock(s, t, turn):
                hid_low(s)
                if exists(s + 1, SUPERBLOCKS):
                    h_low(s + 1)
                if exists(s + 2, SUPERBLOCKS):
                    x_sums(s + 2, t, turn + 1)
                if exists(s + 1, SUPERBLOCKS):
                    residuals(s + 1, 1 - t)

            pool.wait_ge(s_w3, 16 * 7)
            x_sums(0, 0, 0)
            x_sums(1, 1, 0)
            residuals(0, 0)
            h_low(0)
            superblock(0, 0, 0)
            superblock(1, 1, 0)
            with pool.Fori(1, SUPERBLOCKS // 2 - 1) as turn:
                for t in range(2):
                    superblock(2 * turn + t, t, turn)
            for n in range(SUPERBLOCKS - 3, SUPERBLOCKS):
                superblock(n, n % 2, n // 2)

        @block.tensor
        def _(pe):
            def split_matmul(rows, terms, start=True, stop=True):
                passes = [(l[i], r[j]) for i, j in ((0, 0), (0, 1), (1, 0)) for l, r in terms]
                for n, (lhsT, rhs) in enumerate(passes):
                    last = nc.tensor.matmul(rows, lhsT, rhs, start=start and n == 0,
                                            stop=stop and n == len(passes) - 1)
                return last

            def project(n, slot, turn, t, uses):
                pe.wait_ge(s_xlo, n + 1)
                if exists(n - 2, NODE_TILES):
                    pe.wait_ge(s_kvb, n - 1)
                for out_rows, cols in ((bank[2 + t][0:TB, 0:C], (0, C)), (quad[0:TB, t, :], (C, 3 * C))):
                    last = split_matmul(out_rows, [(
                        [xT_parts[:, t, part, k] for part in range(2)],
                        [wqkv_sb[:, part, k * 3 * C + cols[0]:k * 3 * C + cols[1]] for part in range(2)],
                    ) for k in range(KC)])
                last.then_inc(s_mm, 1)

            pe.wait_ge(s_wqkv, 2)
            walk_tiles(pe, project)

            def transposes(n, slot, turn):
                pe.wait_ge(s_oh, n + 1)
                if exists(n - 2, BATCHES):
                    pe.wait_ge(s_ohTc, n - 1)
                for i in range(TILES_PER_BATCH):
                    last = nc.tensor.transpose(bank[slot % 2][:, i * P:(i + 1) * P],
                                               onehot[:, slot, i], ident[:])
                last.then_inc(s_ohT, 1)

            def q_rows(n, slot, turn):
                t, b = divmod(slot, BATCHES_PER_GROUP)
                if b == 0:
                    pe.wait_ge(s_qwin[t], 16 * (turn + 1))
                pe.wait_ge(s_ohTc, n + 1)
                if exists(n - 2, BATCHES):
                    pe.wait_ge(s_prod, n - 1)
                for i in range(TILES_PER_BATCH):
                    rows = quad[:, 2 * (slot % 2) + i // 2, (i % 2) * C:(i % 2 + 1) * C]
                    for part in range(2):
                        last = nc.tensor.matmul(rows, onehotT[:, slot % 2, i * P:(i + 1) * P],
                                                qwin[:, t, part * C:(part + 1) * C],
                                                start=(part == 0), stop=(part == 1))
                last.then_inc(s_qe, 1)

            def sums(n, slot, g):
                t, b = divmod(slot, BATCHES_PER_GROUP)
                pe.wait_ge(s_ev, n + 1)
                if b == 0 and exists(g - 2, GROUPS):
                    pe.wait_ge(s_accc, g - 1)
                for i in range(TILES_PER_BATCH):
                    last = nc.tensor.matmul(bank[2 + t][:, 0:ACC], onehot[:, slot, i], ev[:, b, i],
                                            start=(b == 0 and i == 0), stop=False)
                last.then_inc(s_acc, 1)
                if b == BATCHES_PER_GROUP - 1:
                    if exists(g - 1, GROUPS):
                        pe.wait_ge(s_accc, g)
                    pe.wait_ge(s_csel, g + 1)
                    nc.tensor.matmul(bank[2 + t][:, 0:ACC], carry_sel[:, t], acc_sb[:, 1 - t],
                                     start=False, stop=True).then_inc(s_grp, 1)

            def edges(turn):
                for slot in range(SLOTS):
                    n = SLOTS * turn + slot
                    if exists(n + 1, BATCHES):
                        transposes(n + 1, (slot + 1) % SLOTS, turn)
                    q_rows(n, slot, turn)
                    if exists(n - 2, BATCHES):
                        behind = 2 * turn + (slot - 2) // BATCHES_PER_GROUP
                        sums(n - 2, (slot - 2) % SLOTS, behind)

            pe.wait_ge(s_const, 6)
            pe.wait_ge(s_kvb, NODE_TILES)
            transposes(0, 0, 0)
            turns(pe, edges, TURNS)
            for n in (BATCHES - 2, BATCHES - 1):
                sums(n, n % SLOTS, n // BATCHES_PER_GROUP)

            pe.wait_ge(s_accc, GROUPS)
            pe.wait_ge(s_wparts, 6)

            def transpose_wv(s):
                pe.wait_ge(s3_wv, s + 1)
                if exists(s - 1, SUPERBLOCKS):
                    pe.wait_ge(s3_wvTlo, s)
                for a in range(SB_TILES):
                    for k in range(KC):
                        last = nc.tensor.transpose(bank[0][:, (a * KC + k) * TB:(a * KC + k + 1) * TB],
                                                   wv[0:TB, a, k * P:(k + 1) * P], ident[0:TB, 0:TB])
                last.then_inc(s3_wvT, 1)

            def project_out(s):
                pe.wait_ge(s3_wvThi, s + 1)
                pe.wait_ge(s3_wvTlo, s + 1)
                if exists(s - 1, SUPERBLOCKS):
                    pe.wait_ge(s3_x2, s)
                for a in range(SB_TILES):
                    last = split_matmul(bank[1][0:TB, a * C:(a + 1) * C], [(
                        [wvT[:, part, (a * KC + k) * TB:(a * KC + k + 1) * TB] for part in range(2)],
                        [wp_sb[:, part, k * C:(k + 1) * C] for part in range(2)],
                    ) for k in range(KC)])
                last.then_inc(s3_y, 1)

            def transpose_h(s):
                pe.wait_ge(s3_hn, s + 1)
                if exists(s - 1, SUPERBLOCKS):
                    pe.wait_ge(s3_hTf, s)
                for k in range(KC):
                    for a in range(SB_TILES):
                        last = nc.tensor.transpose(bank[2][:, k * SB + a * TB:k * SB + (a + 1) * TB],
                                                   hn[0:TB, a, k * P:(k + 1) * P], ident[0:TB, 0:TB])
                last.then_inc(s3_hTp, 1)

            def ffn1(s, pairs):
                for pair in pairs:
                    pe.wait_ge(s3_hThi, s + 1)
                    pe.wait_ge(s3_hTlo, s + 1)
                    if pair >= 2 or exists(s - 1, SUPERBLOCKS):
                        pe.wait_ge(s3_gelu, (FC // 2) * s + pair - 1)
                    for j in range(2):
                        f = 2 * pair + j
                        last = split_matmul(quad[:, pair % 2, j * SB:(j + 1) * SB], [(
                            [w1_sb[:, part, k * HIDDEN + f * P:k * HIDDEN + (f + 1) * P] for part in range(2)],
                            [hT[:, part, k * SB:(k + 1) * SB] for part in range(2)],
                        ) for k in range(KC)])
                    last.then_inc(s3_f1, 1)

            def ffn2(s, t, a):
                if a == 0 and exists(s - 2, SUPERBLOCKS):
                    pe.wait_ge(s3_z, s - 1)
                for pair in range(FC // 2):
                    pe.wait_ge(s3_hidlo, (FC // 2) * s + pair + 1)
                    for f in (2 * pair, 2 * pair + 1):
                        last = split_matmul(quad[0:TB, 2 + t, a * C:(a + 1) * C], [(
                            [hid[:, part, f, a * TB:(a + 1) * TB] for part in range(2)],
                            [w2_sb[:, part, f * C:(f + 1) * C] for part in range(2)],
                        )], start=(f == 0), stop=(f == FC - 1))
                last.then_inc(s3_f2, 1)

            def superblock(s, t):
                more = exists(s + 1, SUPERBLOCKS)
                if more:
                    transpose_wv(s + 1)
                ffn1(s, (0,))
                if more:
                    project_out(s + 1)
                ffn1(s, (1, 2, 3))
                ffn2(s, t, 0)
                if more:
                    transpose_h(s + 1)
                ffn2(s, t, 1)

            transpose_wv(0)
            project_out(0)
            transpose_h(0)
            superblock(0, 0)
            superblock(1, 1)
            with pe.Fori(1, SUPERBLOCKS // 2) as turn:
                for t in range(2):
                    superblock(2 * turn + t, t)
            superblock(SUPERBLOCKS - 1, 0)

        @block.scalar
        def _(act):
            def x_high(n, slot, turn):
                act.wait_ge(s_x[slot], 16 * (turn + 1))
                if exists(n - 2, NODE_TILES):
                    act.wait_ge(s_mm, n - 1)
                nc.scalar.activation(xT_parts[:, slot % 2, 0], xT_sb[:, slot], ACT.Copy).then_inc(s_xhi, 1)

            def high_parts(n, slot, turn, t, uses):
                if exists(n + 1, NODE_TILES):
                    x_high(n + 1, (slot + 1) % X_SLOTS, turn + (slot + 1) // X_SLOTS)
                act.wait_ge(s_qfull, n + 1)
                if exists(n - 2, NODE_TILES):
                    act.wait_ge(s_qst[t], 16 * uses)
                nc.scalar.activation(q_out[0:TB, t, 0], q_full[0:TB, t], ACT.Copy).then_inc(s_qhi, 1)

            act.wait_ge(s_w, 32)
            nc.scalar.activation(wqkv_sb[:, 0], wqkv_in[:], ACT.Copy).then_inc(s_wqkv, 1)
            x_high(0, 0, 0)
            walk_tiles(act, high_parts)
            act.wait_ge(s_w3, 16 * 7)
            for w, w_in in ((wp_sb, wp_in), (w1_sb, w1_in), (w2_sb, w2_in)):
                nc.scalar.activation(w[:, 0], w_in[:], ACT.Copy).then_inc(s_wparts, 1)

            def copy_onehotT(n, slot):
                act.wait_ge(s_ohT, n + 1)
                if exists(n - 2, BATCHES):
                    act.wait_ge(s_qe, n - 1)
                nc.scalar.activation(onehotT[:, slot % 2], bank[slot % 2][:], ACT.Copy).then_inc(s_ohTc, 1)

            def exponent(n, slot):
                act.wait_ge(s_clip, n + 1)
                if exists(n - 3, BATCHES):
                    act.wait_ge(s_acc, n - 2)
                nc.scalar.activation(ev[:, slot % BATCHES_PER_GROUP, :, C:ACC],
                                     clipped[:, slot % 2].rearrange("p (i h) -> p i h", h=H),
                                     ACT.Exp, scale=SCALE).then_inc(s_exp, 1)

            def finish_group(g, t):
                act.wait_ge(s_grp, g + 1)
                if exists(g - 2, GROUPS):
                    act.wait_ge(s_aggst, 16 * (g - 1))
                nc.scalar.activation(acc_sb[:, t], bank[2 + t][:, 0:ACC], ACT.Copy).then_inc(s_accc, 1)
                base = act.value_load(bases_sb[0:1, bass.ds(g, 1)], min_val=0, max_val=NODES - 1)
                act.wait_ge(s_accc, g + 1)
                if exists(g - 1, GROUPS):
                    act.wait_ge(s_aggst, 16 * g)
                act.dma_start(agg_dram[bass.ds(base, P), :], acc_sb[:, t]).then_inc(s_aggst, 16)

            def edges(turn):
                for slot in range(SLOTS):
                    n = SLOTS * turn + slot
                    t, b = divmod(slot, BATCHES_PER_GROUP)
                    if exists(n + 1, BATCHES):
                        copy_onehotT(n + 1, (slot + 1) % SLOTS)
                    exponent(n, slot)
                    g = 2 * turn + t - 1
                    if b == BATCHES_PER_GROUP - 1 and exists(g, GROUPS):
                        finish_group(g, 1 - t)

            act.wait_ge(s_const, 6)
            act.wait_ge(s_zero, 32)
            copy_onehotT(0, 0)
            turns(act, edges, TURNS)
            finish_group(GROUPS - 1, (GROUPS - 1) % 2)

            def wvT_high(s):
                act.wait_ge(s3_wvT, s + 1)
                if exists(s - 1, SUPERBLOCKS):
                    act.wait_ge(s3_y, s)
                nc.scalar.activation(wvT[:, 0], bank[0][:, 0:SB_TILES * KC * TB], ACT.Copy)\
                    .then_inc(s3_wvThi, 1)

            def h_high(s):
                act.wait_ge(s3_hTp, s + 1)
                if exists(s - 1, SUPERBLOCKS):
                    act.wait_ge(s3_hTlo, s)
                for k in range(KC):
                    last = nc.scalar.activation(hT_full[:, k * SB:(k + 1) * SB],
                                                bank[2][:, k * SB:(k + 1) * SB], ACT.Identity,
                                                scale=lngb_sb[:, k, 0:1], bias=lngb_sb[:, k, 1:2])
                last.then_inc(s3_hTf, 1)
                act.wait_ge(s3_hTf, s + 1)
                if exists(s - 1, SUPERBLOCKS):
                    act.wait_ge(s3_f1, (FC // 2) * s)
                nc.scalar.activation(hT[:, 0], hT_full[:], ACT.Copy).then_inc(s3_hThi, 1)

            def gelu(s):
                for pair in range(FC // 2):
                    done = (FC // 2) * s + pair
                    act.wait_ge(s3_f1, done + 1)
                    if exists(s - 1, SUPERBLOCKS):
                        act.wait_ge(s3_hidlo, done + 1 - FC // 2)
                    for j in range(2):
                        f = 2 * pair + j
                        last = nc.scalar.activation(hid_full[:, f], quad[:, pair % 2, j * SB:(j + 1) * SB],
                                                    ACT.Gelu, bias=b1_sb[:, f:f + 1])
                    last.then_inc(s3_gelu, 1)
                    act.wait_ge(s3_gelu, done + 1)
                    if pair == 0 and exists(s - 1, SUPERBLOCKS):
                        act.wait_ge(s3_f2, 2 * s)
                    fs = slice(2 * pair, 2 * pair + 2)
                    nc.scalar.activation(hid[:, 0, fs], hid_full[:, fs], ACT.Copy).then_inc(s3_hidhi, 1)

            def superblock(s):
                more = exists(s + 1, SUPERBLOCKS)
                if more:
                    wvT_high(s + 1)
                gelu(s)
                if more:
                    h_high(s + 1)

            wvT_high(0)
            h_high(0)
            superblock(0)
            superblock(1)
            with act.Fori(1, SUPERBLOCKS // 2) as turn:
                for t in range(2):
                    superblock(2 * turn + t)
            superblock(SUPERBLOCKS - 1)

        @block.vector
        def _(dve):
            def x_low(n, slot):
                dve.wait_ge(s_xhi, n + 1)
                nc.vector.tensor_tensor(xT_parts[:, slot % 2, 1], xT_sb[:, slot],
                                        xT_parts[:, slot % 2, 0].bitcast(f32), ALU.subtract).then_inc(s_xlo, 1)

            def biases(n, slot, turn, t, uses):
                if exists(n + 1, NODE_TILES):
                    x_low(n + 1, (slot + 1) % X_SLOTS)
                dve.wait_ge(s_mm, n + 1)
                if exists(n - 2, NODE_TILES):
                    dve.wait_ge(s_qlo, n - 1)
                nc.vector.tensor_tensor(q_full[0:TB, t], bank[2 + t][0:TB, 0:C], bqkv_sb[0:TB, 0:C],
                                        ALU.add).then_inc(s_qfull, 1)
                if exists(n - 2, NODE_TILES):
                    dve.wait_ge(s_kvst[t], 16 * uses)
                nc.vector.tensor_tensor(kv_out[0:TB, t], quad[0:TB, t, :], bqkv_sb[0:TB, C:3 * C],
                                        ALU.add).then_inc(s_kvb, 1)

            dve.wait_ge(s_wqkv, 1)
            nc.vector.tensor_tensor(wqkv_sb[:, 1], wqkv_in[:], wqkv_sb[:, 0].bitcast(f32), ALU.subtract)\
                .then_inc(s_wqkv, 1)
            x_low(0, 0)
            walk_tiles(dve, biases)
            dve.wait_ge(s_wparts, 3)
            for w, w_in in ((wp_sb, wp_in), (w1_sb, w1_in), (w2_sb, w2_in)):
                nc.vector.tensor_tensor(w[:, 1], w_in[:], w[:, 0].bitcast(f32), ALU.subtract)\
                    .then_inc(s_wparts, 1)

            def locate(g, t, turn):
                dve.wait_ge(s_dst[t], 16 * (turn + 1))
                if exists(g - 2, GROUPS):
                    dve.wait_ge(s_oh, BATCHES_PER_GROUP * (g - 1))
                    dve.wait_ge(s_csel, g - 1)
                nc.vector.tensor_tensor(dloc[:, t], dst_sb[:, t],
                                        dst_sb[:, t, TPG:TPG + 1].broadcast_to([P, TPG + 2]),
                                        ALU.subtract).then_inc(s_dloc, 1)

            def select_carry(g, t):
                if exists(g - 2, GROUPS):
                    dve.wait_ge(s_grp, g - 1)
                dve.wait_ge(s_dloc, g + 1)
                nc.vector.tensor_scalar(carry_sel[:, t, 0:1], iota_col[:], dloc[:, t, TPG + 1:TPG + 2], 0.0,
                                        ALU.add, ALU.is_equal).then_inc(s_csel, 1)

            def onehots(n, slot, g, turn):
                t, b = divmod(slot, BATCHES_PER_GROUP)
                if b == 0:
                    locate(g, t, turn)
                    dve.wait_ge(s_dloc, g + 1)
                if exists(n - SLOTS, BATCHES):
                    dve.wait_ge(s_acc, n - SLOTS + 1)
                cols = dloc[:, t, b * TILES_PER_BATCH:(b + 1) * TILES_PER_BATCH]
                nc.vector.tensor_tensor(onehot[:, slot],
                                        iota_row[:].unsqueeze(1).broadcast_to([P, TILES_PER_BATCH, P]),
                                        cols.unsqueeze(2).broadcast_to([P, TILES_PER_BATCH, P]),
                                        ALU.is_equal).then_inc(s_oh, 1)

            def products(n, slot, turn):
                dve.wait_ge(s_kv[slot], 64 * (turn + 1))
                dve.wait_ge(s_qe, n + 1)
                if exists(n - 2, BATCHES):
                    dve.wait_ge(s_score, n - 1)
                h = slot % 2
                nc.vector.tensor_tensor(prod[:, h].rearrange("p (i c) -> p i c", c=C), kv[:, slot, :, 0:C],
                                        quad[:, 2 * h:2 * h + 2, :].rearrange("p a (b c) -> p (a b) c", c=C),
                                        ALU.mult).then_inc(s_prod, 1)

            def scores(n, slot):
                dve.wait_ge(s_prod, n + 1)
                if exists(n - 2, BATCHES):
                    dve.wait_ge(s_clip, n - 1)
                nc.vector.tensor_reduce(score[:, slot % 2], prod[:, slot % 2].rearrange("p (h d) -> p h d", d=HD),
                                        AX.X, ALU.add).then_inc(s_score, 1)

            def clip(n, slot):
                dve.wait_ge(s_score, n + 1)
                if exists(n - 2, BATCHES):
                    dve.wait_ge(s_exp, n - 1)
                nc.vector.tensor_scalar(clipped[:, slot % 2], score[:, slot % 2], CLIP / SCALE, -CLIP / SCALE,
                                        ALU.min, ALU.max).then_inc(s_clip, 1)

            def weight(n, slot, turn):
                dve.wait_ge(s_exp, n + 1)
                b = slot % BATCHES_PER_GROUP
                shape = [P, TILES_PER_BATCH, H, HD]
                nc.vector.tensor_tensor(ev[:, b, :, 0:C].rearrange("p i (h d) -> p i h d", d=HD),
                                        kv[:, slot, :, C:2 * C].rearrange("p i (h d) -> p i h d", d=HD),
                                        ev[:, b, :, C:ACC].unsqueeze(3).broadcast_to(shape),
                                        ALU.mult).then_inc(s_ev, 1)

            def edges(turn):
                for slot in range(SLOTS):
                    n = SLOTS * turn + slot
                    products(n, slot, turn)
                    if exists(n - 1, BATCHES):
                        weight(n - 1, (slot - 1) % SLOTS, turn)
                    scores(n, slot)
                    if exists(n + AHEAD, BATCHES):
                        onehots(n + AHEAD, (slot + AHEAD) % SLOTS,
                                2 * turn + (slot + AHEAD) // BATCHES_PER_GROUP,
                                turn + (slot + AHEAD) // SLOTS)
                    clip(n, slot)
                    t, b = divmod(slot, BATCHES_PER_GROUP)
                    if b == 1:
                        select_carry(2 * turn + t, t)

            dve.wait_ge(s_const, 6)
            for n in range(AHEAD):
                onehots(n, n, 0, 0)
            turns(dve, edges, TURNS)
            weight(BATCHES - 1, SLOTS - 1, TURNS - 1)

            def normalise(s, t, turn):
                dve.wait_ge(s3_in[t], 32 * (turn + 1))
                if exists(s - 1, SUPERBLOCKS):
                    dve.wait_ge(s3_rden, s)
                nc.vector.tensor_scalar(den[0:TB], agg_in[0:TB, t, :, C:ACC], 1e-30, None, ALU.max)\
                    .then_inc(s3_den, 1)
                dve.wait_ge(s3_den, s + 1)
                if exists(s - 1, SUPERBLOCKS):
                    dve.wait_ge(s3_wv, s)
                nc.vector.reciprocal(rden[0:TB], den[0:TB]).then_inc(s3_rden, 1)
                dve.wait_ge(s3_rden, s + 1)
                if exists(s - 1, SUPERBLOCKS):
                    dve.wait_ge(s3_wvT, s)
                nc.vector.tensor_tensor(wv[0:TB].rearrange("p a (h d) -> p a h d", d=HD),
                                        agg_in[0:TB, t, :, 0:C].rearrange("p a (h d) -> p a h d", d=HD),
                                        rden[0:TB].unsqueeze(3).broadcast_to([TB, SB_TILES, H, HD]),
                                        ALU.mult).then_inc(s3_wv, 1)

            def wvT_low(s):
                dve.wait_ge(s3_wvThi, s + 1)
                if exists(s - 1, SUPERBLOCKS):
                    dve.wait_ge(s3_y, s)
                nc.vector.tensor_tensor(wvT[:, 1], bank[0][:, 0:SB_TILES * KC * TB],
                                        wvT[:, 0].bitcast(f32), ALU.subtract).then_inc(s3_wvTlo, 1)

            def residual(s, t):
                dve.wait_ge(s3_y, s + 1)
                dve.wait_ge(s3_xbp, s + 1)
                if exists(s - 2, SUPERBLOCKS):
                    dve.wait_ge(s3_xx, s - 1)
                nc.vector.tensor_tensor(x2[0:TB, t], bank[1][0:TB, 0:SB_TILES * C]
                                        .rearrange("p (a c) -> p a c", c=C), x_bp[0:TB, t],
                                        ALU.add).then_inc(s3_x2, 1)

            def output_sum(s, t):
                dve.wait_ge(s3_f2, 2 * (s + 1))
                dve.wait_ge(s3_xx, s + 1)
                if exists(s - 1, SUPERBLOCKS):
                    dve.wait_ge(s3_out, s)
                nc.vector.tensor_tensor(z[0:TB], quad[0:TB, 2 + t, :].rearrange("p (a c) -> p a c", c=C),
                                        xx[0:TB, t], ALU.add).then_inc(s3_z, 1)

            def layer_norms(s, t, turn):
                first, last_one = exists(s + 1, SUPERBLOCKS), exists(s - 1, SUPERBLOCKS)
                tiles = slice(0 if first else SB_TILES, 2 * SB_TILES if last_one else SB_TILES)
                rows = [(i, x2[0:TB, 1 - t, i] if i < SB_TILES else z[0:TB, i - SB_TILES])
                        for i in range(tiles.start, tiles.stop)]
                if first:
                    dve.wait_ge(s3_x2, s + 2)
                if last_one:
                    dve.wait_ge(s3_z, s)
                if exists(s, SUPERBLOCKS):
                    dve.wait_ge(s3_hn, s + 1)
                if exists(s - 2, SUPERBLOCKS):
                    dve.wait_ge(s3_out, s - 1)
                steps = [0]

                def step(*instructions):
                    instructions[-1].then_inc(s3_ln, 1)
                    steps[0] += 1
                    dve.wait_ge(s3_ln, NORM_STEPS * (s + 1) + steps[0])

                step(*[nc.vector.bn_stats(stats[0:TB, i], v) for i, v in rows])
                dve.sem_inc(s_gate_dve, 1)
                step(*[nc.vector.bn_aggr(mv[0:TB, i], stats[0:TB, i]) for i, v in rows])
                y, v, half, shifted, y2 = (root[0:TB, tiles, c:c + 1] for c in range(5))
                step(nc.vector.tensor_scalar(v, mv[0:TB, tiles, 1:2], EPS, None, ALU.add))
                step(nc.vector.tensor_scalar(half, v, -0.5, None, ALU.mult),
                     nc.vector.tensor_scalar(shifted.bitcast(i32), v.bitcast(i32), 1, None,
                                             ALU.logical_shift_right))
                step(nc.vector.tensor_scalar(y.bitcast(i32), shifted.bitcast(i32), -1.0, ROOT_MAGIC,
                                             ALU.mult, ALU.add))
                for _ in range(NEWTON):
                    step(nc.vector.tensor_tensor(y2, y, y, ALU.mult))
                    step(nc.vector.tensor_tensor(y2, y2, half, ALU.mult))
                    step(nc.vector.scalar_tensor_tensor(y, y2, 1.5, y, ALU.add, ALU.mult))
                assert steps[0] == NORM_STEPS
                if first:
                    if exists(s, SUPERBLOCKS):
                        dve.wait_ge(s3_hTp, s + 1)
                    for i in range(SB_TILES):
                        last = nc.vector.tensor_scalar(hn[0:TB, i], rows[i][1], mv[0:TB, i, 0:1],
                                                       root[0:TB, i, 0:1], ALU.subtract, ALU.mult)
                    last.then_inc(s3_hn, 1)
                if last_one:
                    if exists(s - 3, SUPERBLOCKS):
                        dve.wait_ge(s3_st_out[1 - t], 16 * (turn - 1 + t))
                    for i, v in rows[-SB_TILES:]:
                        last = nc.vector.tensor_scalar(y_out[0:TB, 1 - t, i - SB_TILES], v, mv[0:TB, i, 0:1],
                                                       root[0:TB, i, 0:1], ALU.subtract, ALU.mult)
                    last.then_inc(s3_out, 1)

            def superblock(s, t, turn):
                if exists(s + 1, SUPERBLOCKS):
                    wvT_low(s + 1)
                    residual(s + 1, 1 - t)
                if exists(s - 1, SUPERBLOCKS):
                    output_sum(s - 1, 1 - t)
                layer_norms(s, t, turn)
                if exists(s + 2, SUPERBLOCKS):
                    normalise(s + 2, t, turn + 1)

            normalise(0, 0, 0)
            superblock(-1, 1, -1)
            superblock(0, 0, 0)
            superblock(1, 1, 0)
            superblock(2, 0, 1)
            superblock(3, 1, 1)
            with dve.Fori(2, SUPERBLOCKS // 2 - 1) as turn:
                for t in range(2):
                    superblock(2 * turn + t, t, turn)
            for n in range(SUPERBLOCKS - 3, SUPERBLOCKS + 1):
                superblock(n, n % 2, n // 2)


def kernel(**inputs):
    import numpy as np
    import concourse.bacc as bacc
    from concourse.bass_utils import run_bass_kernel_spmd

    p = "L0_gnn_"
    a = {k: np.asarray(v) for k, v in inputs.items()}
    x = a["x"]
    fill = GROUPS * TPG * P - EDGES
    src = np.concatenate([a["src"], np.zeros(fill, a["src"].dtype)])
    dst = np.concatenate([a["dst"], np.full(fill, NO_NODE, a["dst"].dtype)])

    def by_group(e):
        return np.ascontiguousarray(e.reshape(GROUPS, TPG, P).transpose(0, 2, 1))

    first = np.minimum(np.arange(GROUPS) * TPG * P, (EDGES - 1) // (TPG * P) * TPG * P)
    bases = np.concatenate([np.zeros(1, dst.dtype), dst[first[1:]]])
    before = np.concatenate([np.full(1, -NO_NODE, dst.dtype), bases[:-1]])
    columns = np.stack([bases, before], axis=1)
    edge_dst = np.concatenate([by_group(dst), np.broadcast_to(columns[:, None, :], (GROUPS, P, 2))], axis=2)
    arrays = {
        "xT": x.T, "x": x,
        "w_qkvT": np.concatenate([a[p + "Wq"], a[p + "Wk"], a[p + "Wv"]], axis=0).T,
        "b_qkv": np.concatenate([a[p + "bq"], a[p + "bk"], a[p + "bv"]])[None],
        "wpT": a[p + "Wp"].T, "bp": a[p + "bp"][None],
        "ln_gb": np.stack([a[p + "ln_g"], a[p + "ln_b"]], axis=1).reshape(KC, P, 2).transpose(1, 0, 2),
        "w1T": a[p + "W1"].T, "b1": a[p + "b1"].reshape(FC, P).T,
        "w2T": a[p + "W2"].T, "b2": a[p + "b2"][None],
        "edge_src": by_group(src), "edge_dst": edge_dst, "bases": bases[None],
    }
    nc = bacc.Bacc("TRN2", target_bir_lowering=False, num_devices=1)
    args = []
    arrays = {k: np.ascontiguousarray(v) for k, v in arrays.items()}
    for name, v in arrays.items():
        args.append(nc.dram_tensor(name, v.shape, mybir.dt.from_np(v.dtype), kind="ExternalInput").ap())
    args.append(nc.dram_tensor("out", (NODES, C), mybir.dt.float32, kind="ExternalOutput").ap())
    gnn_program(nc, *args)
    r = run_bass_kernel_spmd(nc, [arrays], core_ids=[0])
    return r.results[0]["out"]
```

```python
import concourse.bass as bass
from concourse import mybir
from contextlib import ExitStack

P = 128
NODES, EDGES, C, H = 6250, 100000, 256, 8
HD = C // H
HIDDEN = 4 * C
TILES_PER_BATCH = 4
BATCHES_PER_GROUP = 3
X_SLOTS = 8
PARTS_SLOTS = 2
OUT_SLOTS = 4
TPG = TILES_PER_BATCH * BATCHES_PER_GROUP
EDGE_TILES = -(-EDGES // P)
GROUPS = -(-EDGE_TILES // TPG)
GROUPS += GROUPS % 2
SLOTS = 2 * BATCHES_PER_GROUP
TURNS = GROUPS // 2
AHEAD = BATCHES_PER_GROUP + 1
BATCHES = max(-(-EDGE_TILES // TILES_PER_BATCH), SLOTS * (TURNS - 1) + AHEAD)
WINDOW_BATCHES = GROUPS * BATCHES_PER_GROUP
ACC = C + H
XCOLS = 125
TB = 125
NODE_TILES = NODES // TB
SB_TILES = 2
SB = TB * SB_TILES
SUPERBLOCKS = NODE_TILES // SB_TILES
KC = C // P
FC = HIDDEN // P
CLIP = 10.0
SCALE = float(HD) ** -0.5
EPS = 1e-5
NEWTON = 3
NORM_STEPS = 5 + 3 * NEWTON
ROOT_MAGIC = float(0x5F3759DF)
WINDOWS = -(-NODES // P)
ORDER_P = 125
NO_NODE = 1 << 20


def gnn_program(nc, xT, x, w_qkvT, b_qkv, wpT, bp, ln_gb, w1T, b1, w2T, b2, edge_src, edge_dst, bases,
                dst_pairs, out):
    f32, f32r, i32 = mybir.dt.float32, mybir.dt.float32r, mybir.dt.int32
    ALU, ACT, AX = mybir.AluOpType, mybir.ActivationFunctionType, mybir.AxisListType

    kv_dram = nc.dram_tensor("kv_rows", [NODES, 2 * C], f32).ap()
    agg_dram = nc.dram_tensor("agg_rows", [NODES + P, ACC], f32).ap()

    ctx, early = ExitStack(), ExitStack()
    with ctx:
        def sb(name, shape, dt=f32, stack=ctx):
            return stack.enter_context(nc.sbuf_tensor(name, shape, dt))

        def sem(name):
            return ctx.enter_context(nc.semaphore(name))

        one_col = sb("one_col", [P, 1])
        iota_row = sb("iota_row", [P, P])
        iota_col = sb("iota_col", [P, 1])
        ident = sb("ident", [P, P])
        wp_sb = sb("wp_sb", [P, 2, KC * C], f32r)
        w1_sb = sb("w1_sb", [P, 2, KC * HIDDEN], f32r)
        w2_sb = sb("w2_sb", [P, 2, FC * C], f32r)
        bp_sb = sb("bp_sb", [P, C])
        b2_sb = sb("b2_sb", [P, C])
        lngb_sb = sb("lngb_sb", [P, KC, 2])
        b1_sb = sb("b1_sb", [P, FC])
        general_flag = sb("general_flag", [1, 1], i32)
        bases_sb = sb("bases_sb", [1, GROUPS + 1], i32)
        wqkv_in = sb("wqkv_in", [P, KC * 3 * C], f32, early)
        wp_in = sb("wp_in", [P, KC * C], f32, early)
        w1_in = sb("w1_in", [P, KC * HIDDEN], f32, early)
        w2_in = sb("w2_in", [P, FC * C], f32, early)
        wqkv_sb = sb("wqkv_sb", [P, 2, KC * 3 * C], f32r, early)
        bqkv_sb = sb("bqkv_sb", [P, 3 * C], f32, early)
        xT_sb = sb("xT_sb", [P, X_SLOTS // 2, KC, 2 * XCOLS], f32, early)
        xT_parts = sb("xT_parts", [P, PARTS_SLOTS, 2, KC, XCOLS], f32r, early)
        kv_out = sb("kv_out", [P, OUT_SLOTS, 2 * C], f32, early)
        src_sb = sb("src_sb", [P, 2, TPG], i32, early)
        dst_sb = sb("dst_sb", [P, 2, TPG + 2], i32, early)
        minus_dloc = sb("minus_dloc", [P, 2, TPG + 2], f32, early)
        distance = sb("distance", [P, TILES_PER_BATCH, P], f32, early)
        xwin_in = sb("xwin_in", [P, 2, KC, P], f32, early)
        xwin_parts = sb("xwin_parts", [P, 2, 2, KC, P], f32r, early)
        q_full = sb("q_full", [P, C], f32, early)
        qwin = sb("qwin", [P, 2, 2 * C], f32r, early)
        kv = sb("kv", [P, SLOTS, TILES_PER_BATCH, 2 * C], f32, early)
        onehot = sb("onehot", [P, SLOTS, TILES_PER_BATCH, P], f32, early)
        onehotT = sb("onehotT", [P, 2, TILES_PER_BATCH * P], f32r, early)
        prod = sb("prod", [P, 2, TILES_PER_BATCH * C], f32, early)
        score = sb("score", [P, 2, TILES_PER_BATCH * H], f32, early)
        clipped = sb("clipped", [P, 2, TILES_PER_BATCH * H], f32, early)
        ev = sb("ev", [P, BATCHES_PER_GROUP, TILES_PER_BATCH, ACC], f32, early)
        carry_sel = sb("carry_sel", [P, 2, P], f32, early)
        acc_sb = sb("acc_sb", [P, 2, ACC], f32, early)
        window_base = sb("window_base", [P, 1], f32, early)
        pairs_sb = sb("pairs_sb", [ORDER_P, 2, EDGES // ORDER_P], i32, early)
        rises = prod[0:ORDER_P, 0, 0:EDGES // ORDER_P]
        least_rise = sb("least_rise", [ORDER_P, 1], f32, early)
        spans = sb("spans", [1, GROUPS], f32, early)
        least = sb("least", [1, 4], f32, early)
        early.close()
        agg_in = sb("agg_in", [P, 2, SB_TILES, ACC])
        x_in = sb("x_in", [P, 2, SB_TILES, C])
        den = sb("den", [P, SB_TILES, H])
        rden = sb("rden", [P, SB_TILES, H])
        wv = sb("wv", [P, SB_TILES, C])
        wvT = sb("wvT", [P, 2, SB_TILES * KC * XCOLS], f32r)
        x_bp = sb("x_bp", [P, 2, SB_TILES, C])
        x_b2 = sb("x_b2", [P, 2, SB_TILES, C])
        x2 = sb("x2", [P, 2, SB_TILES, C])
        xx = sb("xx", [P, 2, SB_TILES, C])
        hn = sb("hn", [P, SB_TILES, C])
        hT_full = sb("hT_full", [P, KC * SB])
        hT = sb("hT", [P, 2, KC * SB], f32r)
        hid_full = sb("hid_full", [P, FC, SB])
        hid = sb("hid", [P, 2, FC, SB], f32r)
        z = sb("z", [P, SB_TILES, C])
        y_out = sb("y_out", [P, 2, SB_TILES, C])
        stats = sb("stats", [P, 2 * SB_TILES, 6])
        mv = sb("mv", [P, 2 * SB_TILES, 2])
        root = sb("root", [P, 2 * SB_TILES, 5])

        bank = [ctx.enter_context(nc.psum_tensor(f"bank{i}", [P, 512], f32)) for i in range(4)]
        quad = ctx.enter_context(nc.psum_tensor("quad", [P, 4, 512], f32))

        s_w = sem("weights_in")
        s_w3 = sem("weights3_in")
        s_id = sem("ident_steps")
        s_const = sem("constants_ready")
        s_bases = sem("bases_in")
        s_wqkv = sem("wqkv_parts")
        s_wparts = sem("weight_parts")
        s_xhi = sem("xT_hi_done")
        s_xlo = sem("xT_lo_done")
        s_x = [sem(f"xT_in{t}") for t in range(X_SLOTS // 2)]
        s_mm = sem("kv_done")
        s_kvb = sem("kv_biased")
        s_kvst = [sem(f"kv_stored{t}") for t in range(OUT_SLOTS)]
        s_src = [sem(f"src_in{t}") for t in range(2)]
        s_dst = [sem(f"dst_in{t}") for t in range(2)]
        s_xwin = [sem(f"xwin_in{t}") for t in range(2)]
        s_xwhi = sem("xwin_hi_done")
        s_xwlo = sem("xwin_lo_done")
        s_qmm = sem("window_q_projected")
        s_qfull = sem("window_q_biased")
        s_qhi = sem("window_q_hi_done")
        s_qlo = sem("window_q_lo_done")
        s_kv = [sem(f"kv_in{t}") for t in range(SLOTS)]
        s_order = sem("order_in")
        s_chk = sem("check_steps")
        s_span = sem("span_steps")
        s_flag = sem("flag_ready")
        g_src = sem("general_sources_in")
        g_dst = sem("general_destinations_in")
        g_xwin = sem("general_window_in")
        g_q = sem("general_window_q_steps")
        g_st = sem("general_sums_stored")
        g_turn = sem("general_batches_done")
        g_win = sem("general_window_ready")
        g_dloc = sem("general_dloc_ready")
        g_kv = [[sem(f"general_kv_in{b}_{i}") for i in range(TILES_PER_BATCH)]
                for b in range(BATCHES_PER_GROUP)]
        g_dist = sem("general_distances_ready")
        g_oh = sem("general_onehot_ready")
        g_ohT = sem("general_onehot_transposed")
        g_ohTc = sem("general_onehotT_copied")
        g_qe = sem("general_q_rows_ready")
        g_prod = sem("general_prod_ready")
        g_score = sem("general_score_ready")
        g_clip = sem("general_clipped_ready")
        g_exp = sem("general_exp_ready")
        g_ev = sem("general_weighted_ready")
        g_acc = sem("general_batch_summed")
        s_dloc = sem("dloc_ready")
        s_csel = sem("carry_sel_ready")
        s_dist = sem("distances_ready")
        s_oh = sem("onehot_ready")
        s_ohT = sem("onehot_transposed")
        s_ohTc = sem("onehotT_copied")
        s_qe = sem("q_rows_ready")
        s_prod = sem("prod_ready")
        s_score = sem("score_ready")
        s_clip = sem("clipped_ready")
        s_exp = sem("exp_ready")
        s_ev = sem("weighted_ready")
        s_acc = sem("batch_summed")
        s_grp = sem("group_summed")
        s_accc = sem("sums_copied")
        s_aggst = sem("sums_stored")
        s3_in = [sem(f"node_rows_in{t}") for t in range(2)]
        s3_den = sem("den_guarded")
        s3_rden = sem("den_inverted")
        s3_wv = sem("wv_ready")
        s3_wvT = sem("wv_transposed")
        s3_wvThi = sem("wvT_hi_done")
        s3_wvTlo = sem("wvT_lo_done")
        s3_xbp = sem("x_bp_ready")
        s3_xb2 = sem("x_b2_ready")
        s3_y = sem("projected")
        s3_x2 = sem("x2_ready")
        s3_xx = sem("xx_ready")
        s3_z = sem("z_ready")
        s3_ln = sem("norm_steps")
        s3_hn = sem("hn_ready")
        s3_hTp = sem("h_transposed")
        s3_hTf = sem("hT_full_done")
        s3_hThi = sem("hT_hi_done")
        s3_hTlo = sem("hT_lo_done")
        s3_f1 = sem("ffn1_done")
        s3_gelu = sem("gelu_done")
        s3_hidhi = sem("hid_hi_done")
        s3_hidlo = sem("hid_lo_done")
        s3_f2 = sem("ffn2_done")
        s3_out = sem("y_out_ready")
        s3_st_out = [sem(f"out_stored{t}") for t in range(2)]

        block = ctx.enter_context(nc.Block())

        s_gate_pool = sem("gate_pool")
        s_gate_dve = sem("gate_dve")
        s_gate_pe = sem("gate_pe")
        s_gate_sp = sem("gate_sp")

        def turns(eng, body, count):
            body(0)
            with eng.Fori(1, count - 1) as turn:
                body(turn)
            body(count - 1)

        def walk_tiles(eng, body):
            def step(turn):
                for i in range(X_SLOTS):
                    if exists(X_SLOTS * turn + i, NODE_TILES):
                        body(X_SLOTS * turn + i, i, turn, i % OUT_SLOTS,
                             X_SLOTS // OUT_SLOTS * turn + i // OUT_SLOTS)

            step(0)
            with eng.Fori(1, NODE_TILES // X_SLOTS) as turn:
                step(turn)
            step(NODE_TILES // X_SLOTS)

        def x_tile(slot):
            return xT_sb[:, slot // 2, :, slot % 2 * TB:(slot % 2 + 1) * TB]

        def exists(n, count):
            return 0 <= n < count if isinstance(n, int) else True

        def general_batches(eng, group_start=None, batch=None, window_start=None, window_end=None):
            with eng.Fori(0, WINDOWS) as w:
                if window_start:
                    window_start(w)
                with eng.Fori(0, GROUPS) as g:
                    if group_start:
                        group_start(w * GROUPS + g, g)
                    for b in range(BATCHES_PER_GROUP if batch else 0):
                        batch(w * GROUPS + g, b)
                if window_end:
                    window_end(w)

        def on_general(eng, path):
            eng.wait_ge(s_flag, 1)
            flag = eng.value_load(general_flag[0:1, 0:1], min_val=0, max_val=1)
            with eng.If(flag > 0):
                path()

        def gather_rows(slot, t, b, signals):
            for i in range(TILES_PER_BATCH):
                col = b * TILES_PER_BATCH + i
                nc.gpsimd.indirect_dma_start(
                    out=kv[:, slot, i, :], out_offset=None, in_=kv_dram,
                    in_offset=bass.IndirectOffsetOnAxis(ap=src_sb[:, t, col:col + 1], axis=0),
                ).then_inc(signals[i], 16)

        def node_distances(t, b):
            for i in range(TILES_PER_BATCH):
                col = b * TILES_PER_BATCH + i
                last = nc.scalar.activation(distance[:, i], iota_row[:], ACT.Abs,
                                            bias=minus_dloc[:, t, col:col + 1])
            return last

        def make_onehots(slot):
            return nc.scalar.activation(onehot[:, slot], distance[:], ACT.Relu, scale=-1.0, bias=one_col[:])

        def window_x_high(t):
            return nc.scalar.activation(xwin_parts[:, t, 0], xwin_in[:, t], ACT.Copy)

        def window_x_low(t):
            return nc.vector.tensor_tensor(xwin_parts[:, t, 1], xwin_in[:, t],
                                           xwin_parts[:, t, 0].bitcast(f32), ALU.subtract)

        def window_q_bias():
            return nc.vector.tensor_tensor(q_full[:], bank[1][:, 0:C], bqkv_sb[:, 0:C], ALU.add)

        def window_q_high(t):
            return nc.scalar.activation(qwin[:, t, 0:C], q_full[:], ACT.Copy)

        def window_q_low(t):
            return nc.vector.tensor_tensor(qwin[:, t, C:2 * C], q_full[:], qwin[:, t, 0:C].bitcast(f32),
                                           ALU.subtract)

        def transposed_bank(slot):
            return bank[slot % BATCHES_PER_GROUP // 2]

        def transpose_onehots(slot):
            for i in range(TILES_PER_BATCH):
                last = nc.tensor.transpose(transposed_bank(slot)[:, i * P:(i + 1) * P], onehot[:, slot, i],
                                           ident[:])
            return last

        def copy_onehots(slot):
            return nc.scalar.activation(onehotT[:, slot % 2], transposed_bank(slot)[:], ACT.Copy)

        def select_q(slot, t):
            for i in range(TILES_PER_BATCH):
                rows = quad[:, 2 * (slot % 2) + i // 2, (i % 2) * C:(i % 2 + 1) * C]
                for part in range(2):
                    last = nc.tensor.matmul(rows, onehotT[:, slot % 2, i * P:(i + 1) * P],
                                            qwin[:, t, part * C:(part + 1) * C],
                                            start=(part == 0), stop=(part == 1))
            return last

        def multiply_qk(slot):
            h = slot % 2
            return nc.vector.tensor_tensor(prod[:, h].rearrange("p (i c) -> p i c", c=C), kv[:, slot, :, 0:C],
                                           quad[:, 2 * h:2 * h + 2, :].rearrange("p a (b c) -> p (a b) c", c=C),
                                           ALU.mult)

        def sum_heads(slot):
            return nc.vector.tensor_reduce(score[:, slot % 2],
                                           prod[:, slot % 2].rearrange("p (h d) -> p h d", d=HD), AX.X, ALU.add)

        def clip_scores(slot):
            return nc.vector.tensor_scalar(clipped[:, slot % 2], score[:, slot % 2], CLIP / SCALE,
                                           -CLIP / SCALE, ALU.min, ALU.max)

        def exponents(slot):
            return nc.scalar.activation(ev[:, slot % BATCHES_PER_GROUP, :, C:ACC],
                                        clipped[:, slot % 2].rearrange("p (i h) -> p i h", h=H),
                                        ACT.Exp, scale=SCALE)

        def weight_v(slot):
            b = slot % BATCHES_PER_GROUP
            return nc.vector.tensor_tensor(ev[:, b, :, 0:C].rearrange("p i (h d) -> p i h d", d=HD),
                                           kv[:, slot, :, C:2 * C].rearrange("p i (h d) -> p i h d", d=HD),
                                           ev[:, b, :, C:ACC].unsqueeze(3)
                                           .broadcast_to([P, TILES_PER_BATCH, H, HD]), ALU.mult)

        @block.sync
        def _(sp):
            sp.dma_start(wqkv_in[:].rearrange("p (k n) -> p k n", k=KC),
                         w_qkvT.rearrange("(k p) n -> p k n", p=P)).then_inc(s_w, 16)
            sp.dma_start(bqkv_sb[:], b_qkv.broadcast_to([P, 3 * C])).then_inc(s_w, 16)

            def load_x(n, slot):
                if exists(n - X_SLOTS, NODE_TILES):
                    sp.wait_ge(s_xlo, n - X_SLOTS + 2)
                sp.dma_start(xT_sb[:, slot // 2],
                             xT[:, bass.ds(n * TB, 2 * TB)].rearrange("(k p) n -> p k n", p=P))\
                    .then_inc(s_x[slot // 2], 16)

            def move_rows(n, slot, turn, t, uses):
                row = n * TB
                sp.wait_ge(s_kvb, n + 1)
                sp.dma_start(kv_dram[bass.ds(row, TB), :], kv_out[0:TB, t]).then_inc(s_kvst[t], 16)
                if slot % 2 == 1 and exists(n + X_SLOTS, NODE_TILES):
                    load_x(n - 1 + X_SLOTS, slot - 1)

            for slot in range(0, X_SLOTS, 2):
                load_x(slot, slot)
            sp.dma_start(bases_sb[:], bases).then_inc(s_bases, 16)
            sp.dma_start(pairs_sb[:], dst_pairs.rearrange("a p n -> p a n")).then_inc(s_order, 16)
            for w, wT, k in ((wp_in, wpT, KC), (w1_in, w1T, KC), (w2_in, w2T, FC)):
                sp.dma_start(w[:].rearrange("p (k n) -> p k n", k=k),
                             wT.rearrange("(k p) n -> p k n", p=P)).then_inc(s_w3, 16)
            sp.dma_start(bp_sb[:], bp.broadcast_to([P, C])).then_inc(s_w3, 16)
            sp.dma_start(b2_sb[:], b2.broadcast_to([P, C])).then_inc(s_w3, 16)
            sp.dma_start(lngb_sb[:], ln_gb).then_inc(s_w3, 16)
            sp.dma_start(b1_sb[:], b1).then_inc(s_w3, 16)
            for n in range(X_SLOTS):
                move_rows(n, n, 0, n % OUT_SLOTS, n // OUT_SLOTS)
            with sp.Fori(1, NODE_TILES // X_SLOTS - 1) as turn:
                for i in range(X_SLOTS):
                    move_rows(X_SLOTS * turn + i, i, turn, i % OUT_SLOTS,
                              X_SLOTS // OUT_SLOTS * turn + i // OUT_SLOTS)
            for n in range(NODE_TILES // X_SLOTS * X_SLOTS - X_SLOTS, NODE_TILES):
                move_rows(n, n % X_SLOTS, n // X_SLOTS, n % OUT_SLOTS, n // OUT_SLOTS)

            def load_group(g, t, turn):
                if exists(turn - 1, TURNS):
                    sp.wait_ge(s_dloc, g - 1)
                sp.dma_start(dst_sb[:, t], edge_dst[bass.ds(g, 1), :, :].rearrange("g p n -> (g p) n"))\
                    .then_inc(s_dst[t], 16)
                base = sp.value_load(bases_sb[0:1, bass.ds(g, 1)], min_val=0, max_val=NODES - 1)
                if exists(turn - 1, TURNS):
                    sp.wait_ge(s_xwlo, g - 1)
                    sp.sem_inc(s_gate_sp, 1)
                sp.dma_start(xwin_in[:, t], xT[:, bass.ds(base, P)].rearrange("(k p) n -> p k n", p=P))\
                    .then_inc(s_xwin[t], 16)
                if exists(turn - 1, TURNS):
                    for b in range(BATCHES_PER_GROUP):
                        sp.wait_ge(s_kv[t * BATCHES_PER_GROUP + b], 64 * turn)
                sp.dma_start(src_sb[:, t], edge_src[bass.ds(g, 1), :, :].rearrange("g p n -> (g p) n"))\
                    .then_inc(s_src[t], 16)

            sp.wait_ge(s_bases, 16)
            load_group(0, 0, 0)
            load_group(1, 1, 0)
            with sp.Fori(1, TURNS) as turn:
                for t in range(2):
                    load_group(2 * turn + t, t, turn)

            sp.wait_ge(s_aggst, 16 * GROUPS)

            def general():
                def window(w):
                    sp.wait_ge(g_turn, w * WINDOW_BATCHES + 1)
                    sp.sem_inc(s_gate_sp, 1)
                    sp.dma_start(xwin_in[:, 0], xT[:, bass.ds(w * P, P)].rearrange("(k p) n -> p k n", p=P))\
                        .then_inc(g_xwin, 16)

                def edges(n, g):
                    sp.wait_ge(g_turn, n * BATCHES_PER_GROUP + 1)
                    sp.dma_start(src_sb[:, 0], edge_src[bass.ds(g, 1), :, :].rearrange("g p n -> (g p) n"))\
                        .then_inc(g_src, 16)
                    sp.dma_start(dst_sb[:, 0], edge_dst[bass.ds(g, 1), :, :].rearrange("g p n -> (g p) n"))\
                        .then_inc(g_dst, 16)

                def store(w):
                    sp.wait_ge(g_turn, (w + 1) * WINDOW_BATCHES + 1)
                    sp.dma_start(agg_dram[bass.ds(w * P, P), :], acc_sb[:, 0]).then_inc(g_st, 16)
                    sp.wait_ge(g_st, 16 * (w + 1))
                    sp.sem_inc(s_gate_sp, 1)

                general_batches(sp, group_start=edges, window_start=window, window_end=store)

            on_general(sp, general)


            def load_nodes(s, t):
                if exists(s - 2, SUPERBLOCKS):
                    sp.wait_ge(s3_wv, s - 1)
                    sp.wait_ge(s3_xb2, s - 1)
                rows = bass.ds(s * SB, SB)
                sp.dma_start(agg_in[0:TB, t], agg_dram[rows, :].rearrange("(a p) n -> p a n", p=TB))\
                    .then_inc(s3_in[t], 16)
                sp.dma_start(x_in[0:TB, t], x[rows, :].rearrange("(a p) n -> p a n", p=TB))\
                    .then_inc(s3_in[t], 16)

            def store_nodes(s, t):
                sp.wait_ge(s3_out, s + 1)
                sp.dma_start(out[bass.ds(s * SB, SB), :].rearrange("(a p) n -> p a n", p=TB),
                             y_out[0:TB, t]).then_inc(s3_st_out[t], 16)

            for s in range(4):
                load_nodes(s, s % 2)
            store_nodes(0, 0)
            load_nodes(4, 0)
            store_nodes(1, 1)
            load_nodes(5, 1)
            with sp.Fori(3, SUPERBLOCKS // 2) as turn:
                for t in range(2):
                    store_nodes(2 * turn + t - 4, t)
                    load_nodes(2 * turn + t, t)
            for s in range(SUPERBLOCKS - 1, SUPERBLOCKS + 4):
                store_nodes(s - 4, s % 2)
                if s < SUPERBLOCKS:
                    load_nodes(s, s % 2)
            sp.wait_ge(s3_st_out[0], 16 * (SUPERBLOCKS // 2 + 1))
            sp.wait_ge(s3_st_out[1], 16 * (SUPERBLOCKS // 2))

        @block.gpsimd
        def _(pool):
            nc.gpsimd.iota(iota_row[:], [[1, P]], base=0, channel_multiplier=0,
                           allow_small_or_imprecise_dtypes=True).then_inc(s_const, 1)
            nc.gpsimd.iota(iota_col[:], [[0, 1]], base=0, channel_multiplier=1,
                           allow_small_or_imprecise_dtypes=True).then_inc(s_const, 1)
            nc.gpsimd.memset(ident[:], 0.0).then_inc(s_id, 1)
            nc.gpsimd.memset(one_col[:], 1.0).then_inc(s_const, 1)
            nc.gpsimd.memset(carry_sel[:], 0.0).then_inc(s_const, 1)
            nc.gpsimd.memset(acc_sb[:], 0.0).then_inc(s_const, 1)
            pool.wait_ge(s_id, 1)
            nc.gpsimd.affine_select(out=ident[:], in_=ident[:], compare_op=ALU.not_equal, fill=1.0,
                                    base=0, pattern=[[-1, P]], channel_multiplier=1).then_inc(s_const, 1)

            for t in range(OUT_SLOTS):
                pool.wait_ge(s_kvst[t], 16 * (-(-(NODE_TILES - t) // OUT_SLOTS)))

            def gather(turn):
                for slot in range(SLOTS):
                    t, b = divmod(slot, BATCHES_PER_GROUP)
                    if b == 0:
                        pool.wait_ge(s_src[t], 16 * (turn + 1))
                    if not exists(SLOTS * turn + slot, BATCHES):
                        continue
                    if exists(turn - 1, TURNS):
                        pool.wait_ge(s_ev, SLOTS * turn + slot - SLOTS + 1)
                    pool.sem_inc(s_gate_pool, 1)
                    gather_rows(slot, t, b, [s_kv[slot]] * TILES_PER_BATCH)

            turns(pool, gather, TURNS)

            def general():
                def edges(n, g):
                    pool.wait_ge(g_src, 16 * (n + 1))

                def batch(n, b):
                    m = n * BATCHES_PER_GROUP + b
                    pool.wait_ge(g_turn, m + 1)
                    pool.sem_inc(s_gate_pool, 1)
                    gather_rows(0, 0, b, g_kv[b])

                general_batches(pool, group_start=edges, batch=batch)

            on_general(pool, general)

            def x_sums(s, t, turn):
                pool.wait_ge(s3_in[t], 32 * (turn + 1))
                if exists(s - 2, SUPERBLOCKS):
                    pool.wait_ge(s3_x2, s - 1)
                for a in range(SB_TILES):
                    last = nc.gpsimd.tensor_tensor(x_bp[0:TB, t, a], x_in[0:TB, t, a], bp_sb[0:TB], ALU.add)
                last.then_inc(s3_xbp, 1)
                if exists(s - 2, SUPERBLOCKS):
                    pool.wait_ge(s3_xx, s - 1)
                for a in range(SB_TILES):
                    last = nc.gpsimd.tensor_tensor(x_b2[0:TB, t, a], x_in[0:TB, t, a], b2_sb[0:TB], ALU.add)
                last.then_inc(s3_xb2, 1)

            def residuals(s, t):
                pool.wait_ge(s3_x2, s + 1)
                pool.wait_ge(s3_xb2, s + 1)
                if exists(s - 2, SUPERBLOCKS):
                    pool.wait_ge(s3_z, s - 1)
                nc.gpsimd.tensor_tensor(xx[0:TB, t], x2[0:TB, t], x_b2[0:TB, t], ALU.add).then_inc(s3_xx, 1)

            def hid_low(s):
                for pair in range(FC // 2):
                    pool.wait_ge(s3_hidhi, (FC // 2) * s + pair + 1)
                    if pair == 0 and exists(s - 1, SUPERBLOCKS):
                        pool.wait_ge(s3_f2, s)
                    fs = slice(2 * pair, 2 * pair + 2)
                    nc.gpsimd.tensor_tensor(hid[:, 1, fs], hid_full[:, fs], hid[:, 0, fs].bitcast(f32),
                                            ALU.subtract).then_inc(s3_hidlo, 1)

            def superblock(s, t, turn):
                hid_low(s)
                if exists(s + 2, SUPERBLOCKS):
                    x_sums(s + 2, t, turn + 1)
                if exists(s + 1, SUPERBLOCKS):
                    residuals(s + 1, 1 - t)

            pool.wait_ge(s_w3, 16 * 7)
            x_sums(0, 0, 0)
            x_sums(1, 1, 0)
            residuals(0, 0)
            superblock(0, 0, 0)
            superblock(1, 1, 0)
            with pool.Fori(1, SUPERBLOCKS // 2 - 1) as turn:
                for t in range(2):
                    superblock(2 * turn + t, t, turn)
            for n in range(SUPERBLOCKS - 3, SUPERBLOCKS):
                superblock(n, n % 2, n // 2)

        @block.tensor
        def _(pe):
            def split_matmul(rows, terms, start=True, stop=True):
                passes = [(l[i], r[j]) for i, j in ((0, 0), (0, 1), (1, 0)) for l, r in terms]
                for n, (lhsT, rhs) in enumerate(passes):
                    last = nc.tensor.matmul(rows, lhsT, rhs, start=start and n == 0,
                                            stop=stop and n == len(passes) - 1)
                return last

            def project(n, slot, turn, t, uses):
                pe.wait_ge(s_xlo, n + 1)
                if exists(n - OUT_SLOTS, NODE_TILES):
                    pe.wait_ge(s_kvb, n - OUT_SLOTS + 1)
                split_matmul(quad[0:TB, t, :], [(
                    [xT_parts[:, slot % PARTS_SLOTS, part, k] for part in range(2)],
                    [wqkv_sb[:, part, k * 3 * C + C:(k + 1) * 3 * C] for part in range(2)],
                ) for k in range(KC)]).then_inc(s_mm, 1)

            def project_window(t):
                return split_matmul(bank[1][:, 0:C], [(
                    [xwin_parts[:, t, part, k] for part in range(2)],
                    [wqkv_sb[:, part, k * 3 * C:k * 3 * C + C] for part in range(2)],
                ) for k in range(KC)])

            pe.wait_ge(s_wqkv, 2)
            walk_tiles(pe, project)

            def transposes(n, slot, turn):
                pe.wait_ge(s_oh, n + 1)
                b, g = slot % BATCHES_PER_GROUP, 2 * turn + slot // BATCHES_PER_GROUP
                if b == 0 and exists(n - 2, BATCHES):
                    pe.wait_ge(s_ohTc, n - 1)
                if b == 1:
                    pe.wait_ge(s_ohTc, n)
                if b == 2:
                    pe.wait_ge(s_qfull, min(g + 2, GROUPS) if isinstance(g, int) else g + 2)
                transpose_onehots(slot).then_inc(s_ohT, 1)

            def window_q(g, t):
                pe.wait_ge(s_xwlo, g + 1)
                if exists(g - 1, GROUPS):
                    pe.wait_ge(s_qfull, g)
                if exists(g - 2, GROUPS):
                    pe.wait_ge(s_ohTc, BATCHES_PER_GROUP * (g - 1))
                project_window(t).then_inc(s_qmm, 1)

            def q_rows(n, slot, turn):
                t, b = divmod(slot, BATCHES_PER_GROUP)
                if b == 0:
                    pe.wait_ge(s_qlo, 2 * turn + t + 1)
                pe.wait_ge(s_ohTc, n + 1)
                if exists(n - 2, BATCHES):
                    pe.wait_ge(s_prod, n - 1)
                select_q(slot, t).then_inc(s_qe, 1)

            def sums(n, slot, g):
                t, b = divmod(slot, BATCHES_PER_GROUP)
                pe.wait_ge(s_ev, n + 1)
                if b == 0 and exists(g - 2, GROUPS):
                    pe.wait_ge(s_accc, g - 1)
                for i in range(TILES_PER_BATCH):
                    last = nc.tensor.matmul(bank[2 + t][:, 0:ACC], onehot[:, slot, i], ev[:, b, i],
                                            start=(b == 0 and i == 0), stop=False)
                last.then_inc(s_acc, 1)
                if b == BATCHES_PER_GROUP - 1 or (isinstance(n, int) and n == BATCHES - 1):
                    if exists(g - 1, GROUPS):
                        pe.wait_ge(s_accc, g)
                    pe.wait_ge(s_csel, g + 1)
                    nc.tensor.matmul(bank[2 + t][:, 0:ACC], carry_sel[:, t], acc_sb[:, 1 - t],
                                     start=False, stop=True).then_inc(s_grp, 1)

            def edges(turn):
                for slot in range(SLOTS):
                    n = SLOTS * turn + slot
                    g = 2 * turn + slot // BATCHES_PER_GROUP
                    if exists(n + 1, BATCHES):
                        transposes(n + 1, (slot + 1) % SLOTS, turn + (slot + 1) // SLOTS)
                    if exists(n, BATCHES):
                        q_rows(n, slot, turn)
                    if slot % BATCHES_PER_GROUP == 2 and exists(g + 2, GROUPS):
                        window_q(g + 2, slot // BATCHES_PER_GROUP)
                    if exists(n - 2, BATCHES):
                        behind = 2 * turn + (slot - 2) // BATCHES_PER_GROUP
                        sums(n - 2, (slot - 2) % SLOTS, behind)

            pe.wait_ge(s_const, 6)
            pe.wait_ge(s_kvb, NODE_TILES)
            window_q(0, 0)
            transposes(0, 0, 0)
            window_q(1, 1)
            turns(pe, edges, TURNS)
            for n in range(SLOTS * TURNS - 2, BATCHES):
                sums(n, n % SLOTS, n // BATCHES_PER_GROUP)

            pe.wait_ge(s_accc, GROUPS - 1)
            pe.wait_ge(s_chk, 2)
            nc.tensor.transpose(bank[2][0:1, 0:ORDER_P], least_rise[:], ident[0:ORDER_P, 0:ORDER_P])\
                .then_inc(s_chk, 1)

            def general():
                def batch(n, b):
                    m = n * BATCHES_PER_GROUP + b
                    pe.wait_ge(g_oh, m + 1)
                    transpose_onehots(0).then_inc(g_ohT, 1)
                    pe.wait_ge(g_ohTc, m + 1)
                    select_q(0, 0).then_inc(g_qe, 1)
                    pe.wait_ge(g_ev, m + 1)
                    for i in range(TILES_PER_BATCH):
                        last = nc.tensor.matmul(bank[2][:, 0:ACC], onehot[:, 0, i], ev[:, 0, i],
                                                start=(i == 0), stop=(i == TILES_PER_BATCH - 1))
                    last.then_inc(g_acc, 1)

                def window(w):
                    pe.wait_ge(g_q, 6 * w + 2)
                    project_window(0).then_inc(g_q, 1)
                    pe.wait_ge(g_q, 6 * w + 6)
                    pe.sem_inc(s_gate_pe, 1)

                general_batches(pe, batch=batch, window_start=window)

            on_general(pe, general)

            pe.wait_ge(s_accc, GROUPS)
            pe.wait_ge(s_wparts, 6)

            def transpose_wv(s):
                pe.wait_ge(s3_wv, s + 1)
                if exists(s - 1, SUPERBLOCKS):
                    pe.wait_ge(s3_wvTlo, s)
                for a in range(SB_TILES):
                    for k in range(KC):
                        last = nc.tensor.transpose(bank[0][:, (a * KC + k) * TB:(a * KC + k + 1) * TB],
                                                   wv[0:TB, a, k * P:(k + 1) * P], ident[0:TB, 0:TB])
                last.then_inc(s3_wvT, 1)

            def project_out(s):
                pe.wait_ge(s3_wvThi, s + 1)
                pe.wait_ge(s3_wvTlo, s + 1)
                if exists(s - 1, SUPERBLOCKS):
                    pe.wait_ge(s3_x2, s)
                for a in range(SB_TILES):
                    last = split_matmul(bank[1][0:TB, a * C:(a + 1) * C], [(
                        [wvT[:, part, (a * KC + k) * TB:(a * KC + k + 1) * TB] for part in range(2)],
                        [wp_sb[:, part, k * C:(k + 1) * C] for part in range(2)],
                    ) for k in range(KC)])
                last.then_inc(s3_y, 1)

            def transpose_h(s):
                pe.wait_ge(s3_hn, s + 1)
                if exists(s - 1, SUPERBLOCKS):
                    pe.wait_ge(s3_hTf, s)
                for k in range(KC):
                    for a in range(SB_TILES):
                        last = nc.tensor.transpose(bank[2][:, k * SB + a * TB:k * SB + (a + 1) * TB],
                                                   hn[0:TB, a, k * P:(k + 1) * P], ident[0:TB, 0:TB])
                last.then_inc(s3_hTp, 1)

            def ffn1(s, pairs):
                for pair in pairs:
                    pe.wait_ge(s3_hThi, s + 1)
                    pe.wait_ge(s3_hTlo, s + 1)
                    if pair >= 2 or exists(s - 1, SUPERBLOCKS):
                        pe.wait_ge(s3_gelu, (FC // 2) * s + pair - 1)
                    for j in range(2):
                        f = 2 * pair + j
                        last = split_matmul(quad[:, pair % 2, j * SB:(j + 1) * SB], [(
                            [w1_sb[:, part, k * HIDDEN + f * P:k * HIDDEN + (f + 1) * P] for part in range(2)],
                            [hT[:, part, k * SB:(k + 1) * SB] for part in range(2)],
                        ) for k in range(KC)])
                    last.then_inc(s3_f1, 1)

            def ffn2(s, pairs):
                for pair in pairs:
                    if pair == 0 and exists(s - 1, SUPERBLOCKS):
                        pe.wait_ge(s3_z, s)
                    pe.wait_ge(s3_hidlo, (FC // 2) * s + pair + 1)
                    for a in range(SB_TILES):
                        for f in (2 * pair, 2 * pair + 1):
                            last = split_matmul(quad[0:TB, 2 + a, 0:C], [(
                                [hid[:, part, f, a * TB:(a + 1) * TB] for part in range(2)],
                                [w2_sb[:, part, f * C:(f + 1) * C] for part in range(2)],
                            )], start=(f == 0), stop=(f == FC - 1))
                    if pair == FC // 2 - 1:
                        last.then_inc(s3_f2, 1)

            def superblock(s):
                more = exists(s + 1, SUPERBLOCKS)
                ffn1(s, (0,))
                if more:
                    project_out(s + 1)
                ffn1(s, (1, 2, 3))
                ffn2(s, (0, 1))
                if more:
                    transpose_h(s + 1)
                ffn2(s, (2,))
                if exists(s + 2, SUPERBLOCKS):
                    transpose_wv(s + 2)
                ffn2(s, (3,))

            transpose_wv(0)
            project_out(0)
            transpose_h(0)
            transpose_wv(1)
            superblock(0)
            superblock(1)
            with pe.Fori(1, SUPERBLOCKS // 2 - 1) as turn:
                for t in range(2):
                    superblock(2 * turn + t)
            for s in range(SUPERBLOCKS - 3, SUPERBLOCKS):
                superblock(s)

        @block.scalar
        def _(act):
            def x_high(n, slot, turn):
                act.wait_ge(s_x[slot // 2], 16 * (turn + 1))
                if exists(n - PARTS_SLOTS, NODE_TILES):
                    act.wait_ge(s_mm, n - PARTS_SLOTS + 1)
                nc.scalar.activation(xT_parts[:, slot % PARTS_SLOTS, 0], x_tile(slot), ACT.Copy).then_inc(s_xhi, 1)

            def high_parts(n, slot, turn, t, uses):
                if exists(n + 1, NODE_TILES):
                    x_high(n + 1, (slot + 1) % X_SLOTS, turn + (slot + 1) // X_SLOTS)

            act.wait_ge(s_w, 32)
            nc.scalar.activation(wqkv_sb[:, 0], wqkv_in[:], ACT.Copy).then_inc(s_wqkv, 1)
            x_high(0, 0, 0)
            walk_tiles(act, high_parts)
            act.wait_ge(s_w3, 16 * 7)
            for w, w_in in ((wp_sb, wp_in), (w1_sb, w1_in), (w2_sb, w2_in)):
                nc.scalar.activation(w[:, 0], w_in[:], ACT.Copy).then_inc(s_wparts, 1)

            def copy_onehotT(n, slot):
                act.wait_ge(s_ohT, n + 1)
                if exists(n - 2, BATCHES):
                    act.wait_ge(s_qe, n - 1)
                copy_onehots(slot).then_inc(s_ohTc, 1)

            def onehots(n, slot, g):
                t, b = divmod(slot, BATCHES_PER_GROUP)
                if b == 0:
                    act.wait_ge(s_dloc, g + 1)
                if exists(n - 1, BATCHES):
                    act.wait_ge(s_oh, n)
                node_distances(t, b).then_inc(s_dist, 1)
                act.wait_ge(s_dist, n + 1)
                if exists(n - SLOTS, BATCHES):
                    act.wait_ge(s_acc, n - SLOTS + 1)
                make_onehots(slot).then_inc(s_oh, 1)

            def x_window_high(g, t, turn):
                act.wait_ge(s_xwin[t], 16 * (turn + 1))
                if exists(g - 2, GROUPS):
                    act.wait_ge(s_qmm, g - 1)
                window_x_high(t).then_inc(s_xwhi, 1)

            def q_high(g, t):
                act.wait_ge(s_qfull, g + 1)
                if exists(g - 2, GROUPS):
                    act.wait_ge(s_qe, BATCHES_PER_GROUP * (g - 1))
                window_q_high(t).then_inc(s_qhi, 1)

            def exponent(n, slot):
                act.wait_ge(s_clip, n + 1)
                if exists(n - 3, BATCHES):
                    act.wait_ge(s_acc, n - 2)
                exponents(slot).then_inc(s_exp, 1)

            def finish_group(g, t):
                act.wait_ge(s_grp, g + 1)
                if exists(g - 2, GROUPS):
                    act.wait_ge(s_aggst, 16 * (g - 1))
                nc.scalar.activation(acc_sb[:, t], bank[2 + t][:, 0:ACC], ACT.Copy).then_inc(s_accc, 1)
                base = act.value_load(bases_sb[0:1, bass.ds(g, 1)], min_val=0, max_val=NODES - 1)
                act.wait_ge(s_accc, g + 1)
                if exists(g - 1, GROUPS):
                    act.wait_ge(s_aggst, 16 * g)
                act.dma_start(agg_dram[bass.ds(base, P), :], acc_sb[:, t]).then_inc(s_aggst, 16)

            def edges(turn):
                for slot in range(SLOTS):
                    n = SLOTS * turn + slot
                    t, b = divmod(slot, BATCHES_PER_GROUP)
                    if b == 1 and exists(2 * turn + t + 1, GROUPS):
                        q_high(2 * turn + t + 1, 1 - t)
                    if b == 0 and exists(2 * turn + t + 2, GROUPS):
                        x_window_high(2 * turn + t + 2, t, turn + 1)
                    if exists(n, BATCHES):
                        exponent(n, slot)
                    if exists(n + 2, BATCHES):
                        copy_onehotT(n + 2, (slot + 2) % SLOTS)
                    if exists(n + AHEAD, BATCHES):
                        onehots(n + AHEAD, (slot + AHEAD) % SLOTS,
                                2 * turn + (slot + AHEAD) // BATCHES_PER_GROUP)
                    g = 2 * turn + t - 1
                    if b == BATCHES_PER_GROUP - 1 and exists(g, GROUPS):
                        finish_group(g, 1 - t)

            act.wait_ge(s_const, 6)
            act.wait_ge(s_bases, 16)
            x_window_high(0, 0, 0)
            x_window_high(1, 1, 0)
            onehots(0, 0, 0)
            q_high(0, 0)
            copy_onehotT(0, 0)
            onehots(1, 1, 0)
            copy_onehotT(1, 1)
            for n in range(2, AHEAD):
                onehots(n, n, n // BATCHES_PER_GROUP)
            turns(act, edges, TURNS)
            finish_group(GROUPS - 1, (GROUPS - 1) % 2)

            def general():
                def window(w):
                    act.wait_ge(g_xwin, 16 * (w + 1))
                    window_x_high(0).then_inc(g_q, 1)
                    act.wait_ge(g_q, 6 * w + 4)
                    window_q_high(0).then_inc(g_q, 1)

                def batch(n, b):
                    m = n * BATCHES_PER_GROUP + b
                    act.wait_ge(g_dloc, n + 1)
                    act.wait_ge(g_turn, m + 1)
                    node_distances(0, b).then_inc(g_dist, 1)
                    act.wait_ge(g_dist, m + 1)
                    make_onehots(0).then_inc(g_oh, 1)
                    act.wait_ge(g_ohT, m + 1)
                    copy_onehots(0).then_inc(g_ohTc, 1)
                    act.wait_ge(g_clip, m + 1)
                    exponents(0).then_inc(g_exp, 1)

                general_batches(act, batch=batch, window_start=window)

            on_general(act, general)

            def wvT_high(s):
                act.wait_ge(s3_wvT, s + 1)
                if exists(s - 1, SUPERBLOCKS):
                    act.wait_ge(s3_y, s)
                nc.scalar.activation(wvT[:, 0], bank[0][:, 0:SB_TILES * KC * TB], ACT.Copy)\
                    .then_inc(s3_wvThi, 1)

            def h_high(s):
                act.wait_ge(s3_hTp, s + 1)
                if exists(s - 1, SUPERBLOCKS):
                    act.wait_ge(s3_hTlo, s)
                for k in range(KC):
                    last = nc.scalar.activation(hT_full[:, k * SB:(k + 1) * SB],
                                                bank[2][:, k * SB:(k + 1) * SB], ACT.Identity,
                                                scale=lngb_sb[:, k, 0:1], bias=lngb_sb[:, k, 1:2])
                last.then_inc(s3_hTf, 1)
                act.wait_ge(s3_hTf, s + 1)
                if exists(s - 1, SUPERBLOCKS):
                    act.wait_ge(s3_f1, (FC // 2) * s)
                nc.scalar.activation(hT[:, 0], hT_full[:], ACT.Copy).then_inc(s3_hThi, 1)

            def gelu(s):
                for pair in range(FC // 2):
                    done = (FC // 2) * s + pair
                    act.wait_ge(s3_f1, done + 1)
                    if exists(s - 1, SUPERBLOCKS):
                        act.wait_ge(s3_hidlo, done + 1 - FC // 2)
                    for j in range(2):
                        f = 2 * pair + j
                        last = nc.scalar.activation(hid_full[:, f], quad[:, pair % 2, j * SB:(j + 1) * SB],
                                                    ACT.Gelu, bias=b1_sb[:, f:f + 1])
                    last.then_inc(s3_gelu, 1)
                    act.wait_ge(s3_gelu, done + 1)
                    if pair == 0 and exists(s - 1, SUPERBLOCKS):
                        act.wait_ge(s3_f2, s)
                    fs = slice(2 * pair, 2 * pair + 2)
                    nc.scalar.activation(hid[:, 0, fs], hid_full[:, fs], ACT.Copy).then_inc(s3_hidhi, 1)

            def superblock(s):
                more = exists(s + 1, SUPERBLOCKS)
                if more:
                    wvT_high(s + 1)
                gelu(s)
                if more:
                    h_high(s + 1)

            wvT_high(0)
            h_high(0)
            superblock(0)
            superblock(1)
            with act.Fori(1, SUPERBLOCKS // 2) as turn:
                for t in range(2):
                    superblock(2 * turn + t)
            superblock(SUPERBLOCKS - 1)

        @block.vector
        def _(dve):
            def x_low(n, slot):
                dve.wait_ge(s_xhi, n + 1)
                nc.vector.tensor_tensor(xT_parts[:, slot % PARTS_SLOTS, 1], x_tile(slot),
                                        xT_parts[:, slot % PARTS_SLOTS, 0].bitcast(f32), ALU.subtract)\
                    .then_inc(s_xlo, 1)

            def biases(n, slot, turn, t, uses):
                if exists(n + 1, NODE_TILES):
                    x_low(n + 1, (slot + 1) % X_SLOTS)
                dve.wait_ge(s_mm, n + 1)
                if exists(n - OUT_SLOTS, NODE_TILES):
                    dve.wait_ge(s_kvst[t], 16 * uses)
                nc.vector.tensor_tensor(kv_out[0:TB, t], quad[0:TB, t, :], bqkv_sb[0:TB, C:3 * C],
                                        ALU.add).then_inc(s_kvb, 1)

            dve.wait_ge(s_wqkv, 1)
            nc.vector.tensor_tensor(wqkv_sb[:, 1], wqkv_in[:], wqkv_sb[:, 0].bitcast(f32), ALU.subtract)\
                .then_inc(s_wqkv, 1)
            x_low(0, 0)
            walk_tiles(dve, biases)
            dve.wait_ge(s_wparts, 3)
            for w, w_in in ((wp_sb, wp_in), (w1_sb, w1_in), (w2_sb, w2_in)):
                nc.vector.tensor_tensor(w[:, 1], w_in[:], w[:, 0].bitcast(f32), ALU.subtract)\
                    .then_inc(s_wparts, 1)

            def locate(g, t, turn):
                dve.wait_ge(s_dst[t], 16 * (turn + 1))
                if exists(g - 2, GROUPS):
                    dve.wait_ge(s_oh, BATCHES_PER_GROUP * (g - 1))
                    dve.wait_ge(s_csel, g - 1)
                nc.vector.tensor_tensor(minus_dloc[:, t],
                                        dst_sb[:, t, TPG:TPG + 1].broadcast_to([P, TPG + 2]),
                                        dst_sb[:, t], ALU.subtract).then_inc(s_dloc, 1)

            def select_carry(g, t):
                if exists(g - 2, GROUPS):
                    dve.wait_ge(s_grp, g - 1)
                dve.wait_ge(s_dloc, g + 1)
                nc.vector.tensor_scalar(carry_sel[:, t, 0:1], iota_col[:],
                                        minus_dloc[:, t, TPG + 1:TPG + 2], 0.0,
                                        ALU.subtract, ALU.is_equal).then_inc(s_csel, 1)

            def x_window_low(g, t):
                dve.wait_ge(s_xwhi, g + 1)
                window_x_low(t).then_inc(s_xwlo, 1)

            def q_bias(g):
                dve.wait_ge(s_qmm, g + 1)
                if exists(g - 1, GROUPS):
                    dve.wait_ge(s_qlo, g)
                window_q_bias().then_inc(s_qfull, 1)

            def q_low(g, t):
                dve.wait_ge(s_qhi, g + 1)
                window_q_low(t).then_inc(s_qlo, 1)

            def products(n, slot, turn):
                dve.wait_ge(s_kv[slot], 64 * (turn + 1))
                dve.wait_ge(s_qe, n + 1)
                if exists(n - 2, BATCHES):
                    dve.wait_ge(s_score, n - 1)
                multiply_qk(slot).then_inc(s_prod, 1)

            def scores(n, slot):
                dve.wait_ge(s_prod, n + 1)
                if exists(n - 2, BATCHES):
                    dve.wait_ge(s_clip, n - 1)
                sum_heads(slot).then_inc(s_score, 1)

            def clip(n, slot):
                dve.wait_ge(s_score, n + 1)
                if exists(n - 2, BATCHES):
                    dve.wait_ge(s_exp, n - 1)
                clip_scores(slot).then_inc(s_clip, 1)

            def weight(n, slot, turn):
                dve.wait_ge(s_exp, n + 1)
                weight_v(slot).then_inc(s_ev, 1)

            def edges(turn):
                for slot in range(SLOTS):
                    n = SLOTS * turn + slot
                    t, b = divmod(slot, BATCHES_PER_GROUP)
                    if exists(n, BATCHES):
                        products(n, slot, turn)
                    if b == 0 and exists(2 * turn + t + 1, GROUPS):
                        q_bias(2 * turn + t + 1)
                    if b == 1 and exists(2 * turn + t + 2, GROUPS):
                        x_window_low(2 * turn + t + 2, t)
                    if exists(n - 1, BATCHES):
                        weight(n - 1, (slot - 1) % SLOTS, turn)
                    if exists(n, BATCHES):
                        scores(n, slot)
                    if b == 1:
                        select_carry(2 * turn + t, t)
                        if exists(2 * turn + t + 1, GROUPS):
                            q_low(2 * turn + t + 1, 1 - t)
                    if exists(n, BATCHES):
                        clip(n, slot)
                    if b == 1 and exists(2 * turn + t + 2, GROUPS):
                        locate(2 * turn + t + 2, t, turn + 1)

            dve.wait_ge(s_const, 6)
            locate(0, 0, 0)
            locate(1, 1, 0)
            x_window_low(0, 0)
            q_bias(0)
            x_window_low(1, 1)
            q_low(0, 0)
            turns(dve, edges, TURNS)
            if BATCHES == SLOTS * TURNS:
                weight(BATCHES - 1, SLOTS - 1, TURNS - 1)

            dve.wait_ge(s_order, 16)
            dve.wait_ge(s_score, BATCHES)
            nc.vector.tensor_tensor(rises, pairs_sb[:, 1], pairs_sb[:, 0], ALU.subtract).then_inc(s_chk, 1)
            dve.wait_ge(s_chk, 1)
            nc.vector.tensor_reduce(least_rise[:], rises, AX.X, ALU.min).then_inc(s_chk, 1)
            dve.wait_ge(s_bases, 16)
            nc.vector.tensor_tensor(spans[:], bases_sb[:, 0:GROUPS], bases_sb[:, 1:GROUPS + 1], ALU.subtract)\
                .then_inc(s_span, 1)
            dve.wait_ge(s_span, 1)
            nc.vector.tensor_reduce(least[:, 0:1], spans[:], AX.X, ALU.min).then_inc(s_span, 1)
            dve.wait_ge(s_chk, 3)
            nc.vector.tensor_reduce(least[:, 1:2], bank[2][0:1, 0:ORDER_P], AX.X, ALU.min).then_inc(s_chk, 1)
            dve.wait_ge(s_span, 2)
            nc.vector.tensor_scalar(least[:, 2:3], least[:, 0:1], float(P - 1), None, ALU.add).then_inc(s_span, 1)
            dve.wait_ge(s_span, 3)
            dve.wait_ge(s_chk, 4)
            nc.vector.tensor_tensor(least[:, 3:4], least[:, 1:2], least[:, 2:3], ALU.min).then_inc(s_span, 1)
            dve.wait_ge(s_span, 4)
            nc.vector.tensor_scalar(general_flag[:], least[:, 3:4], 0.0, None, ALU.is_lt).then_inc(s_flag, 1)

            def general():
                nc.vector.memset(window_base[:], -float(P)).then_inc(g_turn, 1)

                def window(w):
                    dve.wait_ge(g_turn, w * WINDOW_BATCHES + 1)
                    dve.wait_ge(g_q, 6 * w + 1)
                    window_x_low(0).then_inc(g_q, 1)
                    dve.wait_ge(g_q, 6 * w + 3)
                    window_q_bias().then_inc(g_q, 1)
                    dve.wait_ge(g_q, 6 * w + 5)
                    window_q_low(0).then_inc(g_q, 1)
                    nc.vector.memset(acc_sb[:, 0], 0.0).then_inc(g_win, 1)
                    nc.vector.tensor_scalar(window_base[:], window_base[:], float(P), None, ALU.add)\
                        .then_inc(g_win, 1)
                    dve.wait_ge(g_win, 2 * w + 2)
                    dve.sem_inc(s_gate_dve, 1)

                def locate(n, g):
                    dve.wait_ge(g_dst, 16 * (n + 1))
                    nc.vector.tensor_tensor(minus_dloc[:, 0, 0:TPG], window_base[:].broadcast_to([P, TPG]),
                                            dst_sb[:, 0, 0:TPG], ALU.subtract)\
                        .then_inc(g_dloc, 1)

                def batch(n, b):
                    m = n * BATCHES_PER_GROUP + b
                    for arrived in g_kv[b]:
                        dve.wait_ge(arrived, 16 * (n + 1))
                    dve.wait_ge(g_qe, m + 1)
                    multiply_qk(0).then_inc(g_prod, 1)
                    dve.wait_ge(g_prod, m + 1)
                    sum_heads(0).then_inc(g_score, 1)
                    dve.wait_ge(g_score, m + 1)
                    clip_scores(0).then_inc(g_clip, 1)
                    dve.wait_ge(g_exp, m + 1)
                    weight_v(0).then_inc(g_ev, 1)
                    dve.wait_ge(g_acc, m + 1)
                    nc.vector.tensor_tensor(acc_sb[:, 0], acc_sb[:, 0], bank[2][:, 0:ACC], ALU.add)\
                        .then_inc(g_turn, 1)
                    dve.wait_ge(g_turn, m + 2)

                general_batches(dve, group_start=locate, batch=batch, window_start=window)

            on_general(dve, general)

            def normalise(s, t, turn):
                dve.wait_ge(s3_in[t], 32 * (turn + 1))
                if exists(s - 1, SUPERBLOCKS):
                    dve.wait_ge(s3_rden, s)
                nc.vector.tensor_scalar(den[0:TB], agg_in[0:TB, t, :, C:ACC], 1e-30, None, ALU.max)\
                    .then_inc(s3_den, 1)
                dve.wait_ge(s3_den, s + 1)
                if exists(s - 1, SUPERBLOCKS):
                    dve.wait_ge(s3_wv, s)
                nc.vector.reciprocal(rden[0:TB], den[0:TB]).then_inc(s3_rden, 1)
                dve.wait_ge(s3_rden, s + 1)
                if exists(s - 1, SUPERBLOCKS):
                    dve.wait_ge(s3_wvT, s)
                nc.vector.tensor_tensor(wv[0:TB].rearrange("p a (h d) -> p a h d", d=HD),
                                        agg_in[0:TB, t, :, 0:C].rearrange("p a (h d) -> p a h d", d=HD),
                                        rden[0:TB].unsqueeze(3).broadcast_to([TB, SB_TILES, H, HD]),
                                        ALU.mult).then_inc(s3_wv, 1)

            def wvT_low(s):
                dve.wait_ge(s3_wvThi, s + 1)
                if exists(s - 1, SUPERBLOCKS):
                    dve.wait_ge(s3_y, s)
                nc.vector.tensor_tensor(wvT[:, 1], bank[0][:, 0:SB_TILES * KC * TB],
                                        wvT[:, 0].bitcast(f32), ALU.subtract).then_inc(s3_wvTlo, 1)

            def residual(s, t):
                dve.wait_ge(s3_y, s + 1)
                dve.wait_ge(s3_xbp, s + 1)
                if exists(s - 2, SUPERBLOCKS):
                    dve.wait_ge(s3_xx, s - 1)
                nc.vector.tensor_tensor(x2[0:TB, t], bank[1][0:TB, 0:SB_TILES * C]
                                        .rearrange("p (a c) -> p a c", c=C), x_bp[0:TB, t],
                                        ALU.add).then_inc(s3_x2, 1)

            def output_sum(s, t):
                dve.wait_ge(s3_f2, s + 1)
                dve.wait_ge(s3_xx, s + 1)
                if exists(s - 1, SUPERBLOCKS):
                    dve.wait_ge(s3_out, s)
                nc.vector.tensor_tensor(z[0:TB], quad[0:TB, 2:2 + SB_TILES, 0:C],
                                        xx[0:TB, t], ALU.add).then_inc(s3_z, 1)

            def layer_norms(s, t, turn):
                first, last_one = exists(s + 1, SUPERBLOCKS), exists(s - 1, SUPERBLOCKS)
                tiles = slice(0 if first else SB_TILES, 2 * SB_TILES if last_one else SB_TILES)
                rows = [(i, x2[0:TB, 1 - t, i] if i < SB_TILES else z[0:TB, i - SB_TILES])
                        for i in range(tiles.start, tiles.stop)]
                if first:
                    dve.wait_ge(s3_x2, s + 2)
                if last_one:
                    dve.wait_ge(s3_z, s)
                if exists(s, SUPERBLOCKS):
                    dve.wait_ge(s3_hn, s + 1)
                if exists(s - 2, SUPERBLOCKS):
                    dve.wait_ge(s3_out, s - 1)
                steps = [0]

                def step(*instructions):
                    instructions[-1].then_inc(s3_ln, 1)
                    steps[0] += 1
                    dve.wait_ge(s3_ln, NORM_STEPS * (s + 1) + steps[0])

                step(*[nc.vector.bn_stats(stats[0:TB, i], v) for i, v in rows])
                dve.sem_inc(s_gate_dve, 1)
                step(*[nc.vector.bn_aggr(mv[0:TB, i], stats[0:TB, i]) for i, v in rows])
                y, v, half, shifted, y2 = (root[0:TB, tiles, c:c + 1] for c in range(5))
                step(nc.vector.tensor_scalar(v, mv[0:TB, tiles, 1:2], EPS, None, ALU.add))
                step(nc.vector.tensor_scalar(half, v, -0.5, None, ALU.mult),
                     nc.vector.tensor_scalar(shifted.bitcast(i32), v.bitcast(i32), 1, None,
                                             ALU.logical_shift_right))
                step(nc.vector.tensor_scalar(y.bitcast(i32), shifted.bitcast(i32), -1.0, ROOT_MAGIC,
                                             ALU.mult, ALU.add))
                for _ in range(NEWTON):
                    step(nc.vector.tensor_tensor(y2, y, y, ALU.mult))
                    step(nc.vector.tensor_tensor(y2, y2, half, ALU.mult))
                    step(nc.vector.scalar_tensor_tensor(y, y2, 1.5, y, ALU.add, ALU.mult))
                assert steps[0] == NORM_STEPS
                if first:
                    if exists(s, SUPERBLOCKS):
                        dve.wait_ge(s3_hTp, s + 1)
                    for i in range(SB_TILES):
                        last = nc.vector.tensor_scalar(hn[0:TB, i], rows[i][1], mv[0:TB, i, 0:1],
                                                       root[0:TB, i, 0:1], ALU.subtract, ALU.mult)
                    last.then_inc(s3_hn, 1)
                if last_one:
                    if exists(s - 3, SUPERBLOCKS):
                        dve.wait_ge(s3_st_out[1 - t], 16 * (turn - 1 + t))
                    for i, v in rows[-SB_TILES:]:
                        last = nc.vector.tensor_scalar(y_out[0:TB, 1 - t, i - SB_TILES], v, mv[0:TB, i, 0:1],
                                                       root[0:TB, i, 0:1], ALU.subtract, ALU.mult)
                    last.then_inc(s3_out, 1)

            def h_low(s):
                dve.wait_ge(s3_hThi, s + 1)
                if exists(s - 1, SUPERBLOCKS):
                    dve.wait_ge(s3_f1, (FC // 2) * s)
                nc.vector.tensor_tensor(hT[:, 1], hT_full[:], hT[:, 0].bitcast(f32), ALU.subtract)\
                    .then_inc(s3_hTlo, 1)

            def superblock(s, t, turn):
                if exists(s + 1, SUPERBLOCKS):
                    wvT_low(s + 1)
                if exists(s - 1, SUPERBLOCKS):
                    output_sum(s - 1, 1 - t)
                if exists(s + 1, SUPERBLOCKS):
                    residual(s + 1, 1 - t)
                layer_norms(s, t, turn)
                if exists(s + 2, SUPERBLOCKS):
                    normalise(s + 2, t, turn + 1)
                if exists(s + 1, SUPERBLOCKS):
                    h_low(s + 1)

            normalise(0, 0, 0)
            superblock(-1, 1, -1)
            superblock(0, 0, 0)
            superblock(1, 1, 0)
            superblock(2, 0, 1)
            superblock(3, 1, 1)
            with dve.Fori(2, SUPERBLOCKS // 2 - 1) as turn:
                for t in range(2):
                    superblock(2 * turn + t, t, turn)
            for n in range(SUPERBLOCKS - 3, SUPERBLOCKS + 1):
                superblock(n, n % 2, n // 2)


def kernel(**inputs):
    import numpy as np
    import concourse.bacc as bacc
    from concourse.bass_utils import run_bass_kernel_spmd

    p = "L0_gnn_"
    a = {k: np.asarray(v) for k, v in inputs.items()}
    x = a["x"]
    fill = GROUPS * TPG * P - EDGES
    src = np.concatenate([a["src"], np.zeros(fill, a["src"].dtype)])
    dst = np.concatenate([a["dst"], np.full(fill, NO_NODE, a["dst"].dtype)])

    def by_group(e):
        return np.ascontiguousarray(e.reshape(GROUPS, TPG, P).transpose(0, 2, 1))

    first = np.minimum(np.arange(GROUPS) * TPG * P, (EDGES - 1) // (TPG * P) * TPG * P)
    bases = np.concatenate([np.zeros(1, dst.dtype), dst[first[1:]]])
    before = np.concatenate([np.full(1, -NO_NODE, dst.dtype), bases[:-1]])
    columns = np.stack([bases, before], axis=1)
    edge_dst = np.concatenate([by_group(dst), np.broadcast_to(columns[:, None, :], (GROUPS, P, 2))], axis=2)
    arrays = {
        "xT": np.concatenate([x.T, np.zeros((C, P), x.dtype)], axis=1),
        "x": x,
        "w_qkvT": np.concatenate([a[p + "Wq"], a[p + "Wk"], a[p + "Wv"]], axis=0).T,
        "b_qkv": np.concatenate([a[p + "bq"], a[p + "bk"], a[p + "bv"]])[None],
        "wpT": a[p + "Wp"].T, "bp": a[p + "bp"][None],
        "ln_gb": np.stack([a[p + "ln_g"], a[p + "ln_b"]], axis=1).reshape(KC, P, 2).transpose(1, 0, 2),
        "w1T": a[p + "W1"].T, "b1": a[p + "b1"].reshape(FC, P).T,
        "w2T": a[p + "W2"].T, "b2": a[p + "b2"][None],
        "edge_src": by_group(src), "edge_dst": edge_dst,
        "bases": np.concatenate([bases, np.full(1, NODES - 1, bases.dtype)])[None],
        "dst_pairs": np.stack([a["dst"], np.concatenate([a["dst"][1:], a["dst"][-1:]])])
        .reshape(2, ORDER_P, -1),
    }
    nc = bacc.Bacc("TRN2", target_bir_lowering=False, num_devices=1)
    args = []
    arrays = {k: np.ascontiguousarray(v) for k, v in arrays.items()}
    for name, v in arrays.items():
        args.append(nc.dram_tensor(name, v.shape, mybir.dt.from_np(v.dtype), kind="ExternalInput").ap())
    args.append(nc.dram_tensor("out", (NODES, C), mybir.dt.float32, kind="ExternalOutput").ap())
    gnn_program(nc, *args)
    r = run_bass_kernel_spmd(nc, [arrays], core_ids=[0])
    return r.results[0]["out"]
```
